# Optimizing a Trainium2 kernel written in Bass

```python
import numpy as np
import jax
import jax.numpy as jnp

def _softmax(x, axis=-1):
    return jax.nn.softmax(x, axis=axis)

def _gelu(x):
    return jax.nn.gelu(x, approximate=True)

def _silu(x):
    return jax.nn.silu(x)

def _sigmoid(x):
    return jax.nn.sigmoid(x)

def _layernorm(x, axis=-1, eps=1e-05):
    m = jnp.mean(x, axis=axis, keepdims=True)
    v = jnp.var(x, axis=axis, keepdims=True)
    return (x - m) / jnp.sqrt(v + eps)

def _scatter_add(tgt, idx, src, axis=0):
    return tgt.at[idx].add(src)

def _segment_sum(src, seg, n):
    return jax.ops.segment_sum(src, seg, n)
kernel_name = 'mk_seq_postln_d2_jaxref_r4_3e02f0'

def setup_inputs(seed: int=0):
    np.random.seed(seed)
    _w = jnp.asarray

    def _L0_attn_setup():
        import jax, jax.numpy as jnp
        import numpy as np
        from jax import lax
        D = 256
        N = 16
        key = jax.random.key(seed)
        ks = jax.random.split(key, 8)
        sequence = jax.random.normal(ks[0], (2, 512, D), dtype=jnp.float32)
        A = jnp.broadcast_to(-jnp.arange(1, D + 1, dtype=jnp.float32)[:, None], (D, N))
        lim_B = 1.0 / np.sqrt(D)
        W_B = jax.random.uniform(ks[1], (N, D), minval=-lim_B, maxval=lim_B, dtype=jnp.float32)
        b_B = jax.random.uniform(ks[2], (N,), minval=-lim_B, maxval=lim_B, dtype=jnp.float32)
        W_C = jax.random.uniform(ks[3], (N, D), minval=-lim_B, maxval=lim_B, dtype=jnp.float32)
        b_C = jax.random.uniform(ks[4], (N,), minval=-lim_B, maxval=lim_B, dtype=jnp.float32)
        W_Delta = jax.random.uniform(ks[5], (1, D), minval=-lim_B, maxval=lim_B, dtype=jnp.float32)
        b_Delta = jax.random.uniform(ks[6], (1,), minval=-lim_B, maxval=lim_B, dtype=jnp.float32)
        u = jax.random.uniform(ks[7], (1,), dtype=jnp.float32)
        bias_Delta = jnp.log(u / (0.1 - 0.001) + 0.001)
        return {'sequence': sequence, 'A': A, 'W_B': W_B, 'b_B': b_B, 'W_C': W_C, 'b_C': b_C, 'W_Delta': W_Delta, 'b_Delta': b_Delta, 'bias_Delta': bias_Delta}
    _L0_attn_in = _L0_attn_setup()

    def _L0_ffn_setup():
        import jax, jax.numpy as jnp
        import numpy as np
        H, I, E, K = (256, 128, 32, 8)
        B, S = (4, 256)

        def silu(x):
            return x * jax.nn.sigmoid(x)
        key = jax.random.key(seed)
        ks = jax.random.split(key, 14)

        def w(k, shape, fan_in):
            return jax.random.normal(k, shape, jnp.float32) / np.float32(np.sqrt(fan_in))
        return {'hidden_states': jax.random.normal(ks[0], (B, S, H), jnp.float32), 'Wr': w(ks[1], (H, E), H), 'br': jnp.zeros((E,), jnp.float32), 'Wg_s': w(ks[2], (H, I), H), 'bg_s': jnp.zeros((I,), jnp.float32), 'Wu_s': w(ks[3], (H, I), H), 'bu_s': jnp.zeros((I,), jnp.float32), 'Wd_s': w(ks[4], (I, H), I), 'bd_s': jnp.zeros((H,), jnp.float32), 'Wg': w(ks[5], (E, H, I), H), 'bg': jnp.zeros((E, I), jnp.float32), 'Wu': w(ks[6], (E, H, I), H), 'bu': jnp.zeros((E, I), jnp.float32), 'Wd': w(ks[7], (E, I, H), I), 'bd': jnp.zeros((E, H), jnp.float32)}
    _L0_ffn_in = _L0_ffn_setup()

    def _L1_attn_setup():
        import jax, jax.numpy as jnp
        import numpy as np
        B, L, D_MODEL = (4, 512, 256)
        D_INNER, N_STATE, K_CONV, DT_RANK = (512, 16, 4, 64)

        def _silu(v):
            return v * jax.nn.sigmoid(v)
        key = jax.random.key(seed)
        ks = jax.random.split(key, 8)
        g = lambda k, shape, s=0.02: jax.random.normal(k, shape, jnp.float32) * s
        A = jnp.tile(jnp.arange(1, N_STATE + 1, dtype=jnp.float32), (D_INNER, 1))
        return {'x': jax.random.normal(ks[0], (B, L, D_MODEL), jnp.float32), 'in_proj_w': g(ks[1], (2 * D_INNER, D_MODEL)), 'conv_w': g(ks[2], (D_INNER, K_CONV), 0.1), 'conv_b': jnp.zeros((D_INNER,), jnp.float32), 'x_proj_w': g(ks[3], (DT_RANK + 2 * N_STATE, D_INNER)), 'dt_proj_w': g(ks[4], (D_INNER, DT_RANK)), 'dt_proj_b': g(ks[5], (D_INNER,), 0.1), 'A_log': jnp.log(A), 'D_param': jnp.ones((D_INNER,), jnp.float32), 'out_proj_w': g(ks[6], (D_MODEL, D_INNER))}
    _L1_attn_in = _L1_attn_setup()

    def _L1_ffn_setup():
        import jax, jax.numpy as jnp
        import numpy as np
        BS, L, D = (4, 512, 256)
        H, E, K = (8, 16, 2)
        HD = D // H
        I = 1024 // H
        key = jax.random.key(seed)
        ks = jax.random.split(key, 10)
        s = lambda k, shp, fan: jax.random.normal(k, shp, jnp.float32) / np.sqrt(fan)
        return {'x': jax.random.normal(ks[0], (BS, L, D), jnp.float32), 'Wm': s(ks[1], (D, D), D), 'bm': jnp.zeros((D,), jnp.float32), 'expert_emb': jax.random.normal(ks[2], (HD, E), jnp.float32), 'W1': s(ks[3], (E, HD, I), HD), 'b1': jnp.zeros((E, I), jnp.float32), 'W2': s(ks[4], (E, I, HD), I), 'b2': jnp.zeros((E, HD), jnp.float32), 'Wo': s(ks[5], (D, D), D), 'bo': jnp.zeros((D,), jnp.float32)}
    _L1_ffn_in = _L1_ffn_setup()
    _d = {'L0_attn_sequence': _L0_attn_in['sequence'], 'L0_attn_A': _L0_attn_in['A'], 'L0_attn_W_B': _L0_attn_in['W_B'], 'L0_attn_b_B': _L0_attn_in['b_B'], 'L0_attn_W_C': _L0_attn_in['W_C'], 'L0_attn_b_C': _L0_attn_in['b_C'], 'L0_attn_W_Delta': _L0_attn_in['W_Delta'], 'L0_attn_b_Delta': _L0_attn_in['b_Delta'], 'L0_attn_bias_Delta': _L0_attn_in['bias_Delta'], 'L0_ffn_Wr': _L0_ffn_in['Wr'], 'L0_ffn_br': _L0_ffn_in['br'], 'L0_ffn_Wg_s': _L0_ffn_in['Wg_s'], 'L0_ffn_bg_s': _L0_ffn_in['bg_s'], 'L0_ffn_Wu_s': _L0_ffn_in['Wu_s'], 'L0_ffn_bu_s': _L0_ffn_in['bu_s'], 'L0_ffn_Wd_s': _L0_ffn_in['Wd_s'], 'L0_ffn_bd_s': _L0_ffn_in['bd_s'], 'L0_ffn_Wg': _L0_ffn_in['Wg'], 'L0_ffn_bg': _L0_ffn_in['bg'], 'L0_ffn_Wu': _L0_ffn_in['Wu'], 'L0_ffn_bu': _L0_ffn_in['bu'], 'L0_ffn_Wd': _L0_ffn_in['Wd'], 'L0_ffn_bd': _L0_ffn_in['bd'], 'L1_attn_in_proj_w': _L1_attn_in['in_proj_w'], 'L1_attn_conv_w': _L1_attn_in['conv_w'], 'L1_attn_conv_b': _L1_attn_in['conv_b'], 'L1_attn_x_proj_w': _L1_attn_in['x_proj_w'], 'L1_attn_dt_proj_w': _L1_attn_in['dt_proj_w'], 'L1_attn_dt_proj_b': _L1_attn_in['dt_proj_b'], 'L1_attn_A_log': _L1_attn_in['A_log'], 'L1_attn_D_param': _L1_attn_in['D_param'], 'L1_attn_out_proj_w': _L1_attn_in['out_proj_w'], 'L1_ffn_Wm': _L1_ffn_in['Wm'], 'L1_ffn_bm': _L1_ffn_in['bm'], 'L1_ffn_expert_emb': _L1_ffn_in['expert_emb'], 'L1_ffn_W1': _L1_ffn_in['W1'], 'L1_ffn_b1': _L1_ffn_in['b1'], 'L1_ffn_W2': _L1_ffn_in['W2'], 'L1_ffn_b2': _L1_ffn_in['b2'], 'L1_ffn_Wo': _L1_ffn_in['Wo'], 'L1_ffn_bo': _L1_ffn_in['bo']}
    _x0 = _d['L0_attn_sequence']
    _d['L0_attn_sequence'] = jax.random.normal(jax.random.fold_in(jax.random.key(seed), 1), (1, 4096, 256), dtype=_x0.dtype)
    del _x0
    return _d

def reference(L0_attn_sequence, L0_attn_A, L0_attn_W_B, L0_attn_b_B, L0_attn_W_C, L0_attn_b_C, L0_attn_W_Delta, L0_attn_b_Delta, L0_attn_bias_Delta, L0_ffn_Wr, L0_ffn_br, L0_ffn_Wg_s, L0_ffn_bg_s, L0_ffn_Wu_s, L0_ffn_bu_s, L0_ffn_Wd_s, L0_ffn_bd_s, L0_ffn_Wg, L0_ffn_bg, L0_ffn_Wu, L0_ffn_bu, L0_ffn_Wd, L0_ffn_bd, L1_attn_in_proj_w, L1_attn_conv_w, L1_attn_conv_b, L1_attn_x_proj_w, L1_attn_dt_proj_w, L1_attn_dt_proj_b, L1_attn_A_log, L1_attn_D_param, L1_attn_out_proj_w, L1_ffn_Wm, L1_ffn_bm, L1_ffn_expert_emb, L1_ffn_W1, L1_ffn_b1, L1_ffn_W2, L1_ffn_b2, L1_ffn_Wo, L1_ffn_bo):

    def _L0_attn_ref(sequence, A, W_B, b_B, W_C, b_C, W_Delta, b_Delta, bias_Delta):
        import jax, jax.numpy as jnp
        import numpy as np
        from jax import lax
        D = 256
        N = 16
        Bm = sequence @ W_B.T + b_B
        Cm = sequence @ W_C.T + b_C
        Delta = jax.nn.softplus(sequence @ W_Delta.T + b_Delta + bias_Delta)
        A_bar = jnp.exp(A[None, None] * Delta[..., None])
        B_bar = 1.0 / A * (A_bar - 1.0) * Bm[..., None, :]

        def step(state, xs):
            Ab, Bb, x, c = xs
            state = state * Ab + x[..., None] * Bb
            y = jnp.einsum('bdn,bn->bd', state, c)
            return (state, y)
        xs = (jnp.moveaxis(A_bar, 1, 0), jnp.moveaxis(B_bar, 1, 0), jnp.moveaxis(sequence, 1, 0), jnp.moveaxis(Cm, 1, 0))
        init = jnp.zeros(sequence.shape[:-2] + (A.shape[0], A.shape[1]), dtype=sequence.dtype)
        _, ys = lax.scan(step, init, xs)
        return jnp.moveaxis(ys, 0, 1)

    def _L0_ffn_ref(hidden_states, Wr, br, Wg_s, bg_s, Wu_s, bu_s, Wd_s, bd_s, Wg, bg, Wu, bu, Wd, bd):
        import jax, jax.numpy as jnp
        import numpy as np
        H, I, E, K = (256, 128, 32, 8)
        B, S = (4, 256)

        def silu(x):
            return x * jax.nn.sigmoid(x)
        b, s, h = hidden_states.shape
        T = b * s
        x = hidden_states.reshape(T, h)
        logits = jnp.dot(x.astype(jnp.float32), Wr) + br
        aff = jax.nn.sigmoid(logits)
        top_v, top_i = jax.lax.top_k(aff, K)
        top_w = top_v / (jnp.sum(top_v, axis=-1, keepdims=True) + 1e-09)
        top_w = top_w.astype(hidden_states.dtype)
        e_total = Wr.shape[1]
        w_full = jnp.zeros((T, e_total), hidden_states.dtype)
        w_full = w_full.at[jnp.arange(T)[:, None], top_i].set(top_w)
        shared = jnp.dot(silu(jnp.dot(x, Wg_s) + bg_s) * (jnp.dot(x, Wu_s) + bu_s), Wd_s) + bd_s
        gate = silu(jnp.einsum('th,ehi->eti', x, Wg) + bg[:, None, :])
        up = jnp.einsum('th,ehi->eti', x, Wu) + bu[:, None, :]
        down = jnp.einsum('eti,eih->eth', gate * up, Wd) + bd[:, None, :]
        routed = jnp.einsum('te,eth->th', w_full, down)
        return (shared + routed).reshape(b, s, h)

    def _L1_attn_ref(x, in_proj_w, conv_w, conv_b, x_proj_w, dt_proj_w, dt_proj_b, A_log, D_param, out_proj_w):
        import jax, jax.numpy as jnp
        import numpy as np
        B, L, D_MODEL = (4, 512, 256)
        D_INNER, N_STATE, K_CONV, DT_RANK = (512, 16, 4, 64)

        def _silu(v):
            return v * jax.nn.sigmoid(v)
        b, seqlen, _ = x.shape
        x_and_res = jnp.einsum('bld,ed->ble', x, in_proj_w)
        x_in, res = jnp.split(x_and_res, 2, axis=-1)
        xp = jnp.pad(x_in, ((0, 0), (K_CONV - 1, 0), (0, 0)))
        conv = conv_b
        for k in range(K_CONV):
            conv = conv + xp[:, k:k + seqlen, :] * conv_w[:, k]
        u = _silu(conv)
        x_dbl = jnp.einsum('bld,ed->ble', u, x_proj_w)
        dt_in, Bm, Cm = jnp.split(x_dbl, [DT_RANK, DT_RANK + N_STATE], axis=-1)
        dt = jax.nn.softplus(jnp.einsum('blr,er->ble', dt_in, dt_proj_w) + dt_proj_b)
        A = -jnp.exp(A_log)
        dts = jnp.swapaxes(dt, 0, 1)
        Bs = jnp.swapaxes(Bm, 0, 1)
        Cs = jnp.swapaxes(Cm, 0, 1)
        us = jnp.swapaxes(u, 0, 1)

        def step(h, t):
            dt_t, B_t, C_t, u_t = t
            dA = jnp.exp(dt_t[:, :, None] * A)
            h = dA * h + (dt_t * u_t)[:, :, None] * B_t[:, None, :]
            y_t = jnp.einsum('bdn,bn->bd', h, C_t)
            return (h, y_t)
        h0 = jnp.zeros((b, D_INNER, N_STATE), x.dtype)
        _, ys = jax.lax.scan(step, h0, (dts, Bs, Cs, us))
        y = jnp.swapaxes(ys, 0, 1) + u * D_param
        y = y * _silu(res)
        return jnp.einsum('bld,od->blo', y, out_proj_w)

    def _L1_ffn_ref(x, Wm, bm, expert_emb, W1, b1, W2, b2, Wo, bo):
        import jax, jax.numpy as jnp
        import numpy as np
        BS, L, D = (4, 512, 256)
        H, E, K = (8, 16, 2)
        HD = D // H
        I = 1024 // H
        bs, L_, d = x.shape
        h = x @ Wm + bm
        t = h.reshape(bs * L_ * H, HD)
        logits = t @ expert_emb
        w = jax.nn.softmax(logits, axis=-1)
        topw, topi = jax.lax.top_k(w, K)
        hmid = jax.nn.gelu(jnp.einsum('td,edi->tei', t, W1) + b1, approximate=False)
        eo = jnp.einsum('tei,eio->teo', hmid, W2) + b2
        sel = jnp.take_along_axis(eo, topi[:, :, None], axis=1)
        comb = (sel * topw[:, :, None]).sum(axis=1)
        out = comb.reshape(bs, L_, d)
        return out @ Wo + bo
    x = L0_attn_sequence
    x = _layernorm(x + _L0_attn_ref(x, L0_attn_A, L0_attn_W_B, L0_attn_b_B, L0_attn_W_C, L0_attn_b_C, L0_attn_W_Delta, L0_attn_b_Delta, L0_attn_bias_Delta), axis=-1)
    x = _layernorm(x + _L0_ffn_ref(x, L0_ffn_Wr, L0_ffn_br, L0_ffn_Wg_s, L0_ffn_bg_s, L0_ffn_Wu_s, L0_ffn_bu_s, L0_ffn_Wd_s, L0_ffn_bd_s, L0_ffn_Wg, L0_ffn_bg, L0_ffn_Wu, L0_ffn_bu, L0_ffn_Wd, L0_ffn_bd), axis=-1)
    x = _layernorm(x + _L1_attn_ref(x, L1_attn_in_proj_w, L1_attn_conv_w, L1_attn_conv_b, L1_attn_x_proj_w, L1_attn_dt_proj_w, L1_attn_dt_proj_b, L1_attn_A_log, L1_attn_D_param, L1_attn_out_proj_w), axis=-1)
    x = _layernorm(x + _L1_ffn_ref(x, L1_ffn_Wm, L1_ffn_bm, L1_ffn_expert_emb, L1_ffn_W1, L1_ffn_b1, L1_ffn_W2, L1_ffn_b2, L1_ffn_Wo, L1_ffn_bo), axis=-1)
    return x

_drawn_inputs = setup_inputs


def setup_inputs(seed=0):
    import zlib

    import numpy as np

    out = dict(_drawn_inputs(seed))
    spreads = {'L0_ffn_br': (0.0, 0.1),
     'L0_ffn_bg_s': (0.0, 0.1),
     'L0_ffn_bu_s': (0.0, 0.1),
     'L0_ffn_bd_s': (0.0, 0.1),
     'L0_ffn_bg': (0.0, 0.1),
     'L0_ffn_bu': (0.0, 0.1),
     'L0_ffn_bd': (0.0, 0.1),
     'L1_attn_conv_b': (0.0, 0.729),
     'L1_attn_D_param': (1.0, 0.6),
     'L1_ffn_bm': (0.0, 0.1),
     'L1_ffn_b1': (0.0, 0.1),
     'L1_ffn_b2': (0.0, 0.1),
     'L1_ffn_bo': (0.0, 0.1)}
    factors = {'L0_attn_b_B': 3.07,
     'L0_attn_b_C': 2.746,
     'L1_attn_in_proj_w': 5.33,
     'L1_attn_conv_w': 7.359,
     'L1_attn_x_proj_w': 8.0,
     'L1_attn_dt_proj_w': 8.0,
     'L1_attn_dt_proj_b': 8.0,
     'L1_attn_A_log': 8.0,
     'L1_attn_out_proj_w': 5.145}
    for name, (base, spread) in spreads.items():
        noise = np.random.default_rng([zlib.crc32(name.encode()), seed]).standard_normal(out[name].shape)
        drawn = base * np.exp(spread * noise) if base else spread * noise
        out[name] = jnp.asarray(drawn.astype(out[name].dtype))
    for name, factor in factors.items():
        out[name] = (out[name] * factor).astype(out[name].dtype)
    return out
```

```python
from contextlib import ExitStack

import concourse.bass as bass
from concourse import mybir

ALU = mybir.AluOpType
ACT = mybir.ActivationFunctionType
F32 = mybir.dt.float32
AX_X = mybir.AxisListType.X

P = 128
CH = 512
N_STATE = 16
DPT = P // N_STATE
QUAD = 32
NQ = P // QUAD
KPQ = QUAD // DPT
TPB = NQ * KPQ
EPS = 1e-5


class Norm:

    FREE = 2

    def __init__(self, nc, sb, sem, bank, k, xT, bufs=None):
        self.nc, self.avg, self.eps, self.xT = nc, k["avg"], k["eps"], xT
        self.mean_ps = self.var_ps = bank
        self.z, self.zc, self.sq, self.rstd = bufs or (
            sb("norm_z", [P, 2, CH]), sb("norm_zc", [P, 2, CH]), sb("norm_sq", [P, 2, CH]), sb("norm_rstd", [P, CH]))
        self.z_ready = sem("norm_z_ready")
        self.mean_ready = sem("norm_mean_ready")
        self.zc_ready = sem("norm_zc_ready")
        self.sq_ready = sem("norm_sq_ready")
        self.var_ready = sem("norm_var_ready")
        self.log_ready = sem("norm_log_ready")
        self.rstd_ready = sem("norm_rstd_ready")
        self.x_ready = sem("norm_x_ready")

    def add_residual(self, dve, c, half, out_ps, bias=0.0):
        dve.wait_ge(self.zc_ready, c * 2)
        self.nc.vector.scalar_tensor_tensor(out=self.z[:, half], in0=out_ps, scalar=bias,
                                            in1=self.xT[:, half, bass.ts(c, CH)], op0=ALU.add,
                                            op1=ALU.add).then_inc(self.z_ready, 1)

    def mean(self, pe, c):
        pe.wait_ge(self.z_ready, c * 2 + 2 + self.FREE)
        pe.wait_ge(self.log_ready, c)
        self.nc.tensor.matmul(self.mean_ps, self.avg, self.z[:, 0], start=True, stop=False)
        self.nc.tensor.matmul(self.mean_ps, self.avg, self.z[:, 1], start=False,
                              stop=True).then_inc(self.mean_ready, 1)

    def centre(self, dve, c):
        dve.wait_ge(self.mean_ready, c + 1)
        dve.wait_ge(self.x_ready, c * 2)
        for half in range(2):
            self.nc.vector.tensor_tensor(self.zc[:, half], self.z[:, half], self.mean_ps,
                                         ALU.subtract).then_inc(self.zc_ready, 1)

    def square(self, act, c):
        act.wait_ge(self.zc_ready, c * 2 + 2)
        act.wait_ge(self.var_ready, c)
        self.nc.scalar.activation(self.sq[:], self.zc[:], ACT.Square).then_inc(self.sq_ready, 1)

    def variance(self, pe, c):
        pe.wait_ge(self.sq_ready, c + 1)
        self.nc.tensor.matmul(self.var_ps, self.avg, self.sq[:, 0], start=True, stop=False)
        self.nc.tensor.matmul(self.var_ps, self.avg, self.sq[:, 1], start=False,
                              stop=True).then_inc(self.var_ready, 1)

    def deviation(self, act, c):
        act.wait_ge(self.var_ready, c + 1)
        act.wait_ge(self.x_ready, c * 2)
        self.nc.scalar.activation(self.rstd[:], self.var_ps, ACT.Ln,
                                  bias=self.eps).then_inc(self.log_ready, 1)
        act.wait_ge(self.log_ready, c + 1)
        self.nc.scalar.activation(self.rstd[:], self.rstd[:], ACT.Exp, scale=-0.5).then_inc(self.rstd_ready, 1)

    def scale(self, dve, c):
        dve.wait_ge(self.rstd_ready, c + 1)
        for half in range(2):
            self.nc.vector.tensor_tensor(self.xT[:, half, bass.ts(c, CH)], self.zc[:, half],
                                         self.rstd[:], ALU.mult).then_inc(self.x_ready, 1)


def over_chunks(eng, n_chunks, chunk):
    chunk(0, 0, first=True, last=False)
    if n_chunks > 2:
        chunk(1, 1, first=False, last=False)
        if n_chunks > 4:
            with eng.Fori(1, n_chunks // 2 - 1) as i:
                chunk(i * 2, 0, first=False, last=False)
                chunk(i * 2 + 1, 1, first=False, last=False)
        chunk(n_chunks - 2, 0, first=False, last=False)
    chunk(n_chunks - 1, 1, first=False, last=True)


def layer0_scan(nc, xT, k, w):
    T = xT.shape[2]
    NCH = T // CH
    NT = 2 * TPB
    REP, AB, VB, BB, HR, HC = 4, 4, 2, 2, 8, 4
    with ExitStack() as ctx:
        def sb(name, shape):
            return ctx.enter_context(nc.sbuf_tensor("a_" + name, shape, F32))

        def sem(name):
            return ctx.enter_context(nc.semaphore("a_" + name))

        ps = [ctx.enter_context(nc.psum_tensor(f"a_ps{i}", [P, CH], F32)) for i in range(8)]
        rep_ps, y_ps, proj_ps, norm_ps = ps[0:REP], ps[4:6], ps[6], ps[7]
        w_bc = sb("w_bc", [P, 2, 3, P])
        bias = sb("bias", [P, 4])
        step_bias = sb("step_bias", [P, 1])
        a_cols = sb("a_cols", [P, NT])
        inv_a = sb("inv_a", [P, NT])
        x_c = sb("x_c", [P, 2, 2, CH])
        b_rep = sb("b_rep", [P, 2, CH])
        c_rep = sb("c_rep", [P, 2, CH])
        step = sb("step", [P, 2, CH])
        absz = sb("absz", [P, CH])
        e = sb("e", [P, CH])
        err = sb("err", [P, CH])
        ln = sb("ln", [P, CH])
        relu = sb("relu", [P, CH])
        decay = sb("decay", [P, AB, CH])
        v = sb("v", [P, VB, CH])
        drive = sb("drive", [P, BB, CH])
        h = sb("h", [P, HR, CH])
        carry = sb("carry", [P, NT])
        hc = sb("hc", [P, HC, CH])

        loaded = sem("loaded")
        xc_loaded = [sem("xc_loaded0"), sem("xc_loaded1")]
        const_ready = sem("const_ready")
        proj_ready = sem("proj_ready")
        proj_left = sem("proj_left")
        b_ready = sem("b_ready")
        c_ready = sem("c_ready")
        abs_ready = sem("abs_ready")
        e_ready = sem("e_ready")
        ln_ready = sem("ln_ready")
        round_ready = sem("round_ready")
        err_ready = sem("err_ready")
        log_ready = sem("log_ready")
        step_ready = sem("step_ready")
        rep_ready = sem("rep_ready")
        decay_ready = sem("decay_ready")
        v_ready = sem("v_ready")
        drive_ready = sem("drive_ready")
        h_ready = sem("h_ready")
        carry_ready = sem("carry_ready")
        hc_ready = sem("hc_ready")
        y_ready = sem("y_ready")
        norm = Norm(nc, sb, sem, norm_ps[:], k, xT)

        block = ctx.enter_context(nc.Block())
        LOADS = 6 * 16

        @block.sync
        def _(sp):
            sp.dma_start(w_bc[:], w["w_bc"].rearrange("(h p) c m -> p h c m", p=P)).then_inc(loaded, 16)
            sp.dma_start(bias[:, 0:1], w["b_b"]).then_inc(loaded, 16)
            sp.dma_start(bias[:, 1:2], w["b_c"]).then_inc(loaded, 16)
            sp.dma_start(bias[:, 2:3], w["b_step"]).then_inc(loaded, 16)
            sp.dma_start(bias[:, 3:4], w["bias_step"]).then_inc(loaded, 16)
            sp.dma_start(a_cols[:], w["a_cols"]).then_inc(loaded, 16)

            def chunk(c, s, first, last):
                if not (first or (isinstance(c, int) and c == 1)):
                    sp.wait_ge(rep_ready, (c - 1) * NT)
                sp.dma_start(x_c[:, s], w["x"].rearrange("(h p) t -> p h t", p=P)[:, :, bass.ts(c, CH)]
                             ).then_inc(xc_loaded[s], 16)

            over_chunks(sp, NCH, chunk)

        @block.tensor
        def _(pe):
            def project(c, i):
                pe.wait_ge(proj_left, c * 3 + i)
                for half in range(2):
                    last = nc.tensor.matmul(proj_ps[:], w_bc[:, half, i, :], xT[:, half, bass.ts(c, CH)],
                                            start=(half == 0), stop=(half == 1))
                last.then_inc(proj_ready, 1)

            def replicate(c, s, n):
                m, kk, j = n // TPB, n % TPB // NQ, n % NQ
                if n == 0:
                    pe.wait_ge(xc_loaded[s], (c - s) * 8 + 16)
                pe.wait_ge(v_ready, c * NT + n + 1)
                q = slice(QUAD * j, QUAD * j + QUAD)
                nc.tensor.matmul(rep_ps[n % REP][:], k["sel_rep"][q, kk, :], x_c[q, s, m, :],
                                 start=True, stop=True).then_inc(rep_ready, 1)

            def add_states(c, n):
                m, kk, j = n // TPB, n % TPB // NQ, n % NQ
                if n % TPB == 0:
                    pe.wait_ge(norm.z_ready, c * 2 + m + 1)
                pe.wait_ge(hc_ready, c * NT + n + 1 + HR)
                nc.tensor.matmul(y_ps[m][QUAD * j:QUAD * j + QUAD, :], k["sel_sum"][:, kk, :],
                                 hc[:, n % HC, :], start=(kk == 0), stop=(kk == KPQ - 1)
                                 ).then_inc(y_ready, 1)

            def chunk(c, s, first, last):
                for g in range(0, NT, NQ):
                    for n in range(g, g + NQ):
                        replicate(c, s, n)
                    for n in range(g - NQ, g):
                        if n >= 0:
                            add_states(c, n)
                        elif not first:
                            add_states(c - 1, NT + n)
                    if g == 2 * NQ and not first:
                        norm.mean(pe, c - 1)
                    if g == 5 * NQ and not first:
                        norm.variance(pe, c - 1)
                    if g in (2 * NQ, 3 * NQ, 4 * NQ) and not last:
                        project(c + 1, g // NQ - 2)

            pe.wait_ge(loaded, LOADS)
            pe.sem_inc(y_ready, HC)
            for i in range(3):
                project(0, i)
            over_chunks(pe, NCH, chunk)
            for n in range(NT - NQ, NT):
                add_states(NCH - 1, n)
            norm.mean(pe, NCH - 1)
            norm.variance(pe, NCH - 1)

        @block.scalar
        def _(act):
            def spread(c, s, i):
                act.wait_ge(proj_ready, c * 3 + i + 1)
                if i < 2:
                    dst, done = ((b_rep, b_ready), (c_rep, c_ready))[i]
                    nc.scalar.activation(dst[:, s, :], proj_ps[:], ACT.Identity,
                                         bias=bias[:, i:i + 1]).then_inc(done, 1)
                    act.wait_ge(done, c + 1)
                    act.sem_inc(proj_left, 1)
                else:
                    act.wait_ge(step_ready, c)
                    nc.scalar.activation(relu[:], proj_ps[:], ACT.Relu, bias=step_bias[:]
                                         ).then_inc(abs_ready, 1)
                    nc.scalar.activation(absz[:], proj_ps[:], ACT.Abs, bias=step_bias[:]
                                         ).then_inc(abs_ready, 1)
                    act.wait_ge(abs_ready, c * 2 + 2)
                    act.sem_inc(proj_left, 1)
                    nc.scalar.activation(e[:], absz[:], ACT.Exp, scale=-1.0).then_inc(e_ready, 1)
                    act.wait_ge(e_ready, c + 1)
                    nc.scalar.activation(ln[:], e[:], ACT.Ln, bias=1.0).then_inc(ln_ready, 1)
                    nc.scalar.activation(err[:], e[:], ACT.Identity, bias=1.0).then_inc(round_ready, 1)
                    act.wait_ge(round_ready, c * 2 + 1)
                    nc.scalar.activation(err[:], err[:], ACT.Identity, bias=-1.0).then_inc(round_ready, 1)

            def chunk(c, s, first, last):
                act.wait_ge(step_ready, c + 1)
                for n in range(NT):
                    act.wait_ge(h_ready, c * NT + n + 1)
                    nc.scalar.activation(decay[:, n % AB, :], step[:, s, :], ACT.Exp,
                                         scale=a_cols[:, n:n + 1]).then_inc(decay_ready, 1)
                    if n in (12, 16, 20) and not last:
                        if n == 12:
                            act.wait_ge(hc_ready, c * NT + HR)
                        spread(c + 1, 1 - s, n // 4 - 3)
                    if n == 18 and not first:
                        norm.square(act, c - 1)
                    if n == 28 and not first:
                        norm.deviation(act, c - 1)

            act.wait_ge(const_ready, 3)
            for i in range(3):
                spread(0, 0, i)
            over_chunks(act, NCH, chunk)
            norm.square(act, NCH - 1)
            norm.deviation(act, NCH - 1)

        @block.gpsimd
        def _(pool):
            def finish_step(c, s):
                pool.wait_ge(round_ready, c * 2 + 2)
                nc.gpsimd.tensor_tensor(err[:], e[:], err[:], ALU.subtract).then_inc(err_ready, 1)
                pool.wait_ge(err_ready, c + 1)
                pool.wait_ge(ln_ready, c + 1)
                nc.gpsimd.tensor_tensor(ln[:], ln[:], err[:], ALU.add).then_inc(log_ready, 1)
                pool.wait_ge(log_ready, c + 1)
                nc.gpsimd.tensor_tensor(step[:, s, :], ln[:], relu[:], ALU.add).then_inc(step_ready, 1)

            def chunk(c, s, first, last):
                pool.wait_ge(c_ready, c + 1)
                for n in range(NT):
                    pool.wait_ge(h_ready, c * NT + n + 1 + AB)
                    pool.wait_ge(y_ready, c * NT + n + 1)
                    nc.gpsimd.tensor_tensor(hc[:, n % HC, :], h[:, n % HR, :], c_rep[:, s, :],
                                            ALU.mult).then_inc(hc_ready, 1)
                    if n == 22 and not last:
                        finish_step(c + 1, 1 - s)

            pool.sem_inc(hc_ready, HR)
            finish_step(0, 0)
            over_chunks(pool, NCH, chunk)

        @block.vector
        def _(dve):
            def scaled_input(c, s, n):
                if n == 0:
                    dve.wait_ge(b_ready, c + 1)
                dve.wait_ge(rep_ready, c * NT + n + 1)
                dve.wait_ge(drive_ready, c * NT + n + 1)
                nc.vector.scalar_tensor_tensor(out=v[:, n % VB, :], in0=rep_ps[n % REP][:],
                                               scalar=inv_a[:, n:n + 1], in1=b_rep[:, s, :],
                                               op0=ALU.mult, op1=ALU.mult).then_inc(v_ready, 1)

            def driving(c, n):
                dve.wait_ge(v_ready, c * NT + n + 1 + REP)
                dve.wait_ge(decay_ready, c * NT + n + 1)
                dve.wait_ge(h_ready, c * NT + n + 1 + AB - BB)
                nc.vector.scalar_tensor_tensor(out=drive[:, n % BB, :], in0=decay[:, n % AB, :],
                                               scalar=-1.0, in1=v[:, n % VB, :],
                                               op0=ALU.add, op1=ALU.mult).then_inc(drive_ready, 1)

            def scan(c, n):
                dve.wait_ge(drive_ready, c * NT + n + 1 + VB)
                dve.wait_ge(hc_ready, c * NT + n + 1)
                if n % NQ == 0:
                    dve.wait_ge(carry_ready, c * (NT // NQ) + n // NQ + 1)
                nc.vector.tensor_tensor_scan(out=h[:, n % HR, :], data0=decay[:, n % AB, :],
                                             data1=drive[:, n % BB, :], initial=carry[:, n:n + 1],
                                             op0=ALU.mult, op1=ALU.add).then_inc(h_ready, 1)

            def keep_last_states(c, g):
                dve.wait_ge(h_ready, c * NT + g + NQ + AB)
                nc.vector.tensor_copy(carry[:, g:g + NQ], h[:, g % HR:g % HR + NQ, CH - 1]
                                      ).then_inc(carry_ready, 1)

            def residual(c):
                for half in range(2):
                    dve.wait_ge(y_ready, c * NT + TPB * (half + 1) + HC)
                    norm.add_residual(dve, c, half, y_ps[half][:])

            def chunk(c, s, first, last):
                for n in range(NT + 3):
                    if n < NT:
                        scaled_input(c, s, n)
                    if 0 <= n - 1 < NT:
                        driving(c, n - 1)
                    if 0 <= n - 2 < NT:
                        scan(c, n - 2)
                    if n >= 3 and (n - 3) % NQ == NQ - 1:
                        keep_last_states(c, n - 3 - (NQ - 1))
                    if not first:
                        if n == 5:
                            residual(c - 1)
                        if n == 14:
                            norm.centre(dve, c - 1)
                        if n == 32:
                            norm.scale(dve, c - 1)

            dve.wait_ge(loaded, LOADS)
            nc.vector.reciprocal(inv_a[:], a_cols[:]).then_inc(const_ready, 1)
            nc.vector.tensor_tensor(step_bias[:], bias[:, 2:3], bias[:, 3:4], ALU.add).then_inc(const_ready, 1)
            nc.vector.memset(carry[:], 0.0).then_inc(const_ready, 1)
            dve.wait_ge(const_ready, 3)
            dve.sem_inc(v_ready, REP)
            dve.sem_inc(drive_ready, VB)
            dve.sem_inc(h_ready, AB)
            dve.sem_inc(carry_ready, NT // NQ)
            dve.sem_inc(norm.z_ready, norm.FREE)
            over_chunks(dve, NCH, chunk)
            residual(NCH - 1)
            norm.centre(dve, NCH - 1)
            norm.scale(dve, NCH - 1)


def layer0_experts(nc, xT, k, w):
    T = xT.shape[2]
    NCH, NB = T // CH, T // P
    BPC = CH // P
    E1, _, PACK = w["experts"].shape
    D, NE, K = 2 * P, E1 - 1, 8
    F32R = mybir.dt.float32r
    WCOLS = 3 * D
    IN = 4
    LAG = 2
    WBUF = 3
    assert E1 % WBUF == 0 and E1 // WBUF >= 3
    with ExitStack() as ctx:
        def sb(name, shape, dt=F32):
            return ctx.enter_context(nc.sbuf_tensor("b_" + name, shape, dt))

        def sem(name):
            return ctx.enter_context(nc.semaphore("b_" + name))

        ps = [ctx.enter_context(nc.psum_tensor(f"b_ps{i}", [P, CH], F32)) for i in range(8)]
        pack = sb("pack", [P, WBUF, PACK])
        parts = [sb(f"pack_{n}", [P, WBUF, WCOLS], F32R) for n in ("high", "low")]
        gate_w = [[a[:, b, 0:D].rearrange("p (h i) -> p h i", h=2) for a in parts] for b in range(WBUF)]
        up_w = [[a[:, b, D:2 * D].rearrange("p (h i) -> p h i", h=2) for a in parts] for b in range(WBUF)]
        down_w = [[a[:, b, 2 * D:3 * D] for a in parts] for b in range(WBUF)]
        x_parts = [sb(f"x_{n}", [P, 2, T], F32R) for n in ("high", "low")]
        PARTS = ((0, 0), (0, 1), (1, 0))
        gate_b = [pack[:, b, 3 * D:3 * D + 1] for b in range(WBUF)]
        up_b = [pack[:, b, 3 * D + 1:3 * D + 2] for b in range(WBUF)]
        router_w = sb("router_w", [P, 2, NE])
        router_b = sb("router_b", [NE, 1])
        down_b = sb("down_b", [E1, D])
        aff = sb("aff", [P, 2, BPC, NE])
        top = sb("top", [P, 2, BPC, K])
        rest = sb("rest", [P, 2, BPC, NE])
        total = sb("total", [P, 2, BPC])
        w_c = sb("w_c", [P, 2, BPC, E1])
        w_all = sb("w_all", [P, NB, E1])
        acc = sb("acc", [P, NB, D])
        silu = sb("silu", [P, 2, CH])
        inner = sb("inner", [P, 2, CH])
        in_parts = [sb(f"inner_{n}", [P, IN, CH], F32R) for n in ("high", "low")]
        scratch = sb("scratch", [P, 2, CH])
        logit_t, w_t = scratch[0:NE], inner[0:E1]

        loaded = sem("loaded")
        ones_ready = sem("ones_ready")
        logit_ready = sem("logit_ready")
        logit_kept = sem("logit_kept")
        logit_turned = sem("logit_turned")
        aff_ready = sem("aff_ready")
        top_ready = sem("top_ready")
        rest_ready = sem("rest_ready")
        total_ready = sem("total_ready")
        picked = sem("picked")
        w_ready = sem("w_ready")
        w_kept = sem("w_kept")
        w_turned = sem("w_turned")
        wt_ready = sem("wt_ready")
        bias_ready = sem("bias_ready")
        acc_started = sem("acc_started")
        pack_loaded = [sem(f"pack_loaded{b}") for b in range(WBUF)]
        x_high = sem("x_high")
        x_low = sem("x_low")
        w_high = sem("w_high")
        w_low = sem("w_low")
        in_high = sem("in_high")
        in_low = sem("in_low")
        gate_ready = sem("gate_ready")
        up_ready = sem("up_ready")
        silu_ready = sem("silu_ready")
        inner_ready = sem("inner_ready")
        down_ready = sem("down_ready")
        acc_ready = sem("acc_ready")
        turned = sem("turned")
        norm = Norm(nc, sb, sem, ps[7][:], k, xT,
                    (inner[:], sb("norm_zc", [P, 2, CH]), scratch[:], silu[:, 0]))

        block = ctx.enter_context(nc.Block())
        LOADS = 3 * 16
        x_of = lambda half, c: xT[:, half, c * CH:(c + 1) * CH]

        def over_experts(eng, expert):
            for b in range(WBUF):
                expert(b, 0, b)
            with eng.Fori(1, E1 // WBUF - 1) as i:
                for b in range(WBUF):
                    expert(i * WBUF + b, i, b)
            for b in range(WBUF):
                expert(E1 - WBUF + b, E1 // WBUF - 1, b)

        def before(e, b, c, n):
            if c >= n:
                return e, b, c - n
            return None if isinstance(e, int) and e == 0 else (e - 1, (b - 1) % WBUF, c - n + NCH)

        @block.sync
        def _(sp):
            sp.dma_start(router_w[:], w["router_w"].rearrange("(h p) e -> p h e", p=P)).then_inc(loaded, 16)
            sp.dma_start(router_b[:], w["router_b"]).then_inc(loaded, 16)
            sp.dma_start(down_b[:], w["down_b"]).then_inc(loaded, 16)

            def expert(e, i, b):
                if not (isinstance(e, int) and e < WBUF):
                    sp.wait_ge(acc_ready, (e - WBUF + 1) * NCH * BPC + 2 * BPC)
                sp.dma_start(pack[:, b], w["experts"][bass.ds(e, 1)].rearrange("o p n -> p (o n)")
                             ).then_inc(pack_loaded[b], 16)

            over_experts(sp, expert)

        @block.tensor
        def _(pe):
            pe.wait_ge(loaded, LOADS)

            def logits(c):
                pe.wait_ge(logit_kept, c)
                for half in range(2):
                    last = nc.tensor.matmul(ps[0][0:NE, :], router_w[:, half, :], x_of(half, c),
                                            start=(half == 0), stop=(half == 1))
                last.then_inc(logit_ready, 1)

            def turn_logits(c):
                pe.wait_ge(logit_kept, c + 1)
                pe.wait_ge(aff_ready, c)
                for b in range(BPC):
                    last = nc.tensor.transpose(ps[1][:, b * NE:(b + 1) * NE],
                                               logit_t[:, c % 2, b * P:(b + 1) * P], k["ident"][0:NE, 0:NE])
                last.then_inc(logit_turned, 1)

            def start_sums(c):
                pe.wait_ge(w_ready, (c + 1) * BPC)
                pe.wait_ge(wt_ready, c)
                for b in range(BPC):
                    last = nc.tensor.transpose(ps[2][0:E1, b * P:(b + 1) * P], w_c[:, c % 2, b, :], k["ident"])
                last.then_inc(w_turned, 1)
                pe.wait_ge(wt_ready, c + 1)
                pe.wait_ge(acc_started, c * 2)
                for b in range(BPC):
                    last = nc.tensor.matmul(ps[3 + b // 2][:, b % 2 * D:b % 2 * D + D],
                                            w_t[:, c % 2, b * P:(b + 1) * P], down_b[:], start=True, stop=True)
                last.then_inc(bias_ready, 1)

            for c in range(NCH + 2):
                if c < NCH:
                    logits(c)
                if 1 <= c <= NCH:
                    turn_logits(c - 1)
                if c >= 2:
                    start_sums(c - 2)
            pe.wait_ge(acc_started, NCH * 2)

            def gate_up(e, b, c):
                q = e * NCH + c
                if c == 0:
                    pe.wait_ge(w_high, e + 1)
                    pe.wait_ge(w_low, e + 1)
                if isinstance(e, int) and e == 0:
                    pe.wait_ge(x_high, c + 1)
                    pe.wait_ge(x_low, c + 1)
                for weights, bank, left, done in ((gate_w, ps[c % 2], silu_ready, gate_ready),
                                                  (up_w, ps[2 + c % 2], inner_ready, up_ready)):
                    pe.wait_ge(left, q + 1)
                    for n, (half, (i, j)) in enumerate((half, p) for half in range(2) for p in PARTS):
                        last = nc.tensor.matmul(bank[:], weights[b][i][:, half, :],
                                                x_parts[j][:, half, c * CH:(c + 1) * CH],
                                                start=(n == 0), stop=(n == 5))
                    last.then_inc(done, 1)

            def down(e, b, c):
                q = e * NCH + c
                pe.wait_ge(in_high, q + 1)
                pe.wait_ge(in_low, q + 1)
                pe.wait_ge(acc_ready, (q + 1) * BPC)
                for t in range(BPC):
                    for n, (i, j) in enumerate(PARTS):
                        last = nc.tensor.matmul(ps[4 + 2 * (c % 2) + t // 2][:, t % 2 * D:t % 2 * D + D],
                                                in_parts[i][:, c % IN, t * P:(t + 1) * P], down_w[b][j],
                                                start=(n == 0), stop=(n == 2))
                last.then_inc(down_ready, 1)

            def expert(e, i, b):
                for c in range(NCH):
                    gate_up(e, b, c)
                    if at := before(e, b, c, LAG):
                        down(*at)

            pe.sem_inc(down_ready, IN)
            over_experts(pe, expert)
            for n in range(LAG):
                down(E1 - 1, (E1 - 1) % WBUF, NCH - LAG + n)
            def turn(c):
                if c >= 2:
                    pe.wait_ge(norm.z_ready, (c - 1) * 2 + norm.FREE)
                for half in range(2):
                    for b in range(BPC):
                        last = nc.tensor.transpose(ps[c % 2 * 2 + half][:, b * P:(b + 1) * P],
                                                   acc[:, c * BPC + b, half * P:(half + 1) * P], k["ident"])
                    last.then_inc(turned, 1)

            pe.wait_ge(acc_ready, E1 * NCH * BPC + 2 * BPC)
            turn(0)
            for c in range(NCH):
                norm.mean(pe, c)
                if c + 1 < NCH:
                    turn(c + 1)
                norm.variance(pe, c)

        @block.scalar
        def _(act):
            act.wait_ge(loaded, LOADS)

            def keep_logits(c):
                act.wait_ge(logit_ready, c + 1)
                if c >= 2:
                    act.wait_ge(logit_turned, c - 1)
                nc.scalar.activation(logit_t[:, c % 2, :], ps[0][0:NE, :], ACT.Identity,
                                     bias=router_b[:]).then_inc(logit_kept, 1)

            def affinity(c):
                act.wait_ge(logit_turned, c + 1)
                if c >= 2:
                    act.wait_ge(picked, c - 1)
                nc.scalar.activation(aff[:, c % 2], ps[1][:, 0:BPC * NE].rearrange("p (b e) -> p b e", b=BPC),
                                     ACT.Sigmoid).then_inc(aff_ready, 1)

            def keep_weights(c):
                act.wait_ge(w_turned, c + 1)
                if c >= 2:
                    act.wait_ge(bias_ready, c - 1)
                nc.scalar.copy(w_t[:, c % 2, :], ps[2][0:E1, :]).then_inc(wt_ready, 1)

            for c in range(NCH + 2):
                if c < NCH:
                    nc.scalar.copy(x_parts[0][:, :, c * CH:(c + 1) * CH], xT[:, :, c * CH:(c + 1) * CH]
                                   ).then_inc(x_high, 1)
                    keep_logits(c)
                if 1 <= c <= NCH:
                    affinity(c - 1)
                if c >= 2:
                    keep_weights(c - 2)

            def split_weights(e, i, b):
                act.wait_ge(pack_loaded[b], i * 16 + 16)
                if not (isinstance(e, int) and e < WBUF):
                    act.wait_ge(down_ready, (e - WBUF + 1) * NCH + IN)
                nc.scalar.copy(parts[0][:, b, :], pack[:, b, 0:WCOLS]).then_inc(w_high, 1)

            def split_inner(e, b, c):
                q = e * NCH + c
                act.wait_ge(inner_ready, q + 1 + 2)
                act.wait_ge(down_ready, q + 1)
                nc.scalar.copy(in_parts[0][:, c % IN, :], inner[:, c % 2, :]).then_inc(in_high, 1)

            def expert(e, i, b):
                for c in range(NCH):
                    q = e * NCH + c
                    act.wait_ge(gate_ready, q + 1)
                    act.wait_ge(inner_ready, q + 1)
                    nc.scalar.activation(silu[:, c % 2, :], ps[c % 2][:], ACT.Silu,
                                         bias=gate_b[b]).then_inc(silu_ready, 1)
                    if at := before(e, b, c, 1):
                        split_inner(*at)
                    if c == NCH // 2 and not (isinstance(e, int) and e == E1 - 1):
                        if b + 1 < WBUF:
                            split_weights(e + 1, i, b + 1)
                        else:
                            split_weights(e + 1, i + 1, 0)

            split_weights(0, 0, 0)
            act.sem_inc(silu_ready, 2)
            over_experts(act, expert)
            split_inner(E1 - 1, (E1 - 1) % WBUF, NCH - 1)
            for c in range(NCH):
                norm.square(act, c)
                norm.deviation(act, c)

        @block.gpsimd
        def _(pool):
            for c in range(NCH):
                pool.wait_ge(x_high, c + 1)
                cols = slice(c * CH, (c + 1) * CH)
                nc.gpsimd.tensor_tensor(x_parts[1][:, :, cols], xT[:, :, cols],
                                        x_parts[0][:, :, cols].bitcast(F32), ALU.subtract).then_inc(x_low, 1)

            def split_weights(e, b):
                pool.wait_ge(w_high, e + 1)
                nc.gpsimd.tensor_tensor(parts[1][:, b, :], pack[:, b, 0:WCOLS], parts[0][:, b, :].bitcast(F32),
                                        ALU.subtract).then_inc(w_low, 1)

            def expert(e, i, b):
                for c in range(NCH):
                    pool.wait_ge(in_high, e * NCH + c + 1)
                    nc.gpsimd.tensor_tensor(in_parts[1][:, c % IN, :], inner[:, c % 2, :],
                                            in_parts[0][:, c % IN, :].bitcast(F32), ALU.subtract
                                            ).then_inc(in_low, 1)
                    if c == NCH // 2 and not (isinstance(e, int) and e == E1 - 1):
                        split_weights(e + 1, (b + 1) % WBUF)

            split_weights(0, 0)
            over_experts(pool, expert)

        @block.vector
        def _(dve):
            nc.vector.memset(w_c[:, :, :, NE:E1], 1.0).then_inc(ones_ready, 1)
            dve.wait_ge(ones_ready, 1)
            dve.sem_inc(inner_ready, 2)
            dve.sem_inc(acc_ready, 2 * BPC)
            dve.sem_inc(norm.z_ready, norm.FREE)

            def weigh(c):
                s = c % 2
                dve.wait_ge(aff_ready, c + 1)
                for b in range(BPC):
                    nc.vector.max(top[:, s, b, :], aff[:, s, b, :]).then_inc(top_ready, 1)
                dve.wait_ge(top_ready, (c + 1) * BPC)
                for b in range(BPC):
                    nc.vector.match_replace(out=rest[:, s, b, :], in_to_replace=top[:, s, b, :],
                                            in_values=aff[:, s, b, :], imm_value=0.0).then_inc(rest_ready, 1)
                nc.vector.reduce_sum(total[:, s, :], top[:, s], axis=AX_X).then_inc(total_ready, 1)
                dve.wait_ge(total_ready, c * 3 + 1)
                nc.vector.tensor_scalar(total[:, s, :], total[:, s, :], 1e-9, None, ALU.add).then_inc(total_ready, 1)
                dve.wait_ge(total_ready, c * 3 + 2)
                nc.vector.reciprocal(total[:, s, :], total[:, s, :]).then_inc(total_ready, 1)
                dve.wait_ge(rest_ready, (c + 1) * BPC)
                nc.vector.tensor_tensor(rest[:, s], aff[:, s], rest[:, s], ALU.subtract).then_inc(picked, 1)
                dve.wait_ge(total_ready, c * 3 + 3)
                dve.wait_ge(picked, c + 1)
                if c >= 2:
                    dve.wait_ge(w_turned, c - 1)
                    dve.wait_ge(w_kept, c - 1)
                for b in range(BPC):
                    nc.vector.tensor_scalar(w_c[:, s, b, 0:NE], rest[:, s, b, :], total[:, s, b:b + 1], None,
                                            ALU.mult).then_inc(w_ready, 1)
                dve.wait_ge(w_ready, (c + 1) * BPC)
                nc.vector.tensor_copy(w_all[:, c * BPC:(c + 1) * BPC, :], w_c[:, s]).then_inc(w_kept, 1)

            def start_acc(c):
                dve.wait_ge(bias_ready, c + 1)
                for i in range(BPC // 2):
                    b = c * BPC + 2 * i
                    nc.vector.tensor_copy(acc[:, b:b + 2, :], ps[3 + i][:].rearrange("p (b d) -> p b d", b=2)
                                          ).then_inc(acc_started, 1)

            for c in range(NCH + 1):
                if c < NCH:
                    weigh(c)
                if c >= 1:
                    start_acc(c - 1)
            dve.wait_ge(w_kept, NCH)
            dve.wait_ge(acc_started, 2 * NCH)

            def gate_times_up(e, b, c):
                q = e * NCH + c
                dve.wait_ge(up_ready, q + 1)
                dve.wait_ge(silu_ready, q + 1 + 2)
                if not (isinstance(e, int) and e == 0 and c < 2):
                    dve.wait_ge(in_low, q - 1)
                nc.vector.scalar_tensor_tensor(out=inner[:, c % 2, :], in0=ps[2 + c % 2][:], scalar=up_b[b],
                                               in1=silu[:, c % 2, :], op0=ALU.add, op1=ALU.mult
                                               ).then_inc(inner_ready, 1)

            def accumulate(e, b, c):
                q = e * NCH + c
                dve.wait_ge(down_ready, q + 1 + IN)
                if not (isinstance(e, int) and e == 0):
                    dve.wait_ge(acc_ready, (q - NCH + 1) * BPC + 2 * BPC)
                for t in range(BPC):
                    tb = c * BPC + t
                    nc.vector.scalar_tensor_tensor(
                        out=acc[:, tb, :], in0=ps[4 + 2 * (c % 2) + t // 2][:, t % 2 * D:t % 2 * D + D],
                        scalar=w_all[:, tb, bass.ds(e, 1)], in1=acc[:, tb, :], op0=ALU.mult, op1=ALU.add
                    ).then_inc(acc_ready, 1)

            def expert(e, i, b):
                for c in range(NCH):
                    gate_times_up(e, b, c)
                    if at := before(e, b, c, LAG):
                        accumulate(*at)

            over_experts(dve, expert)
            for n in range(LAG):
                accumulate(E1 - 1, (E1 - 1) % WBUF, NCH - LAG + n)

            def residual(c):
                for half in range(2):
                    dve.wait_ge(turned, c * 2 + half + 1)
                    norm.add_residual(dve, c, half, ps[c % 2 * 2 + half][:])

            residual(0)
            for c in range(NCH):
                norm.centre(dve, c)
                if c + 1 < NCH:
                    residual(c + 1)
                norm.scale(dve, c)


def layer1_scan(nc, xT, k, w):
    T = xT.shape[2]
    NCH = T // CH
    D, DI = 2 * P, w["out_w"].shape[0]
    NM = DI // P
    RANK = w["dt_w"].shape[0]
    TAPS = w["conv_w"].shape[2]
    HALO = TAPS - 1
    PAIR = 2
    NU = N_STATE * NM // PAIR
    NT = NU * PAIR
    DEC, VB, HR, HC, BC = 4, 2, 4, 2, 4
    ITEMS = 2 * NM + 1 + NM
    X_DBL = 2 * NM
    UPN = NM // PAIR
    with ExitStack() as ctx:
        def sb(name, shape):
            return ctx.enter_context(nc.sbuf_tensor("c_" + name, shape, F32))

        def sem(name):
            return ctx.enter_context(nc.semaphore("c_" + name))

        ps = [ctx.enter_context(nc.psum_tensor(f"c_ps{i}", [P, CH], F32)) for i in range(7)]
        y_ps, work_ps, norm_ps = ps[0:4], ps[4:6], ps[6]
        bc_dram = nc.dram_tensor("c_bc_scratch", (2, 2, N_STATE, CH), F32, kind="Internal").ap()
        in_w = sb("in_w", [P, 2, 2 * DI])
        x_w = sb("x_w", [P, NM, RANK + 2 * N_STATE])
        dt_w = sb("dt_w", [RANK, DI])
        out_w = sb("out_w", [P, NM, D])
        conv_w = sb("conv_w", [P, NM, TAPS])
        vecs = sb("vecs", [P, 3, NM])
        conv_b, dt_b, d_skip = vecs[:, 0], vecs[:, 1], vecs[:, 2]
        a_cols = sb("a_cols", [P, NT])
        xin = sb("xin", [P, NM, HALO + CH])
        u = sb("u", [P, 2, NM, CH])
        gate = sb("gate", [P, 2, NM, CH])
        dt = sb("dt", [P, 2, NM, CH])
        dtu = sb("dtu", [P, 2, NM, CH])
        e = sb("e", [P, NM, CH])
        x_dbl = sb("x_dbl", [RANK + 2 * N_STATE, CH])
        b_rep = sb("b_rep", [P, BC, CH])
        c_rep = sb("c_rep", [P, BC, CH])
        decay = sb("decay", [P, DEC, CH])
        v = sb("v", [P, VB, PAIR, CH])
        h = sb("h", [P, HR, PAIR, CH])
        hc = sb("hc", [P, HC, PAIR, CH])
        carry = sb("carry", [P, NT])

        loaded = sem("loaded")
        a_ready = sem("a_ready")
        work_ready = sem("work_ready")
        work_left = sem("work_left")
        relu_ready = sem("relu_ready")
        tap0_ready = sem("tap0_ready")
        taps_ready = sem("taps_ready")
        halo_ready = sem("halo_ready")
        u_ready = sem("u_ready")
        gate_ready = sem("gate_ready")
        e_ready = sem("e_ready")
        w_ready = sem("w_ready")
        err_ready = sem("err_ready")
        ln_ready = sem("ln_ready")
        log_ready = sem("log_ready")
        dt_ready = sem("dt_ready")
        dtu_ready = sem("dtu_ready")
        bc_stored = sem("bc_stored")
        b_loaded = [sem(f"b_loaded{i}") for i in range(BC)]
        c_loaded = [sem(f"c_loaded{i}") for i in range(BC)]
        decay_ready = sem("decay_ready")
        v_ready = sem("v_ready")
        h_ready = sem("h_ready")
        carry_ready = sem("carry_ready")
        hc_ready = sem("hc_ready")
        y_ready = sem("y_ready")
        skip_ready = sem("skip_ready")
        gated = sem("gated")
        out_ready = sem("out_ready")
        norm = Norm(nc, sb, sem, norm_ps[:], k, xT)

        block = ctx.enter_context(nc.Block())
        LOADS = 7 * 16

        @block.sync
        def _(sp):
            sp.dma_start(in_w[:], w["in_w"].rearrange("(h p) n -> p h n", p=P)).then_inc(loaded, 16)
            sp.dma_start(x_w[:], w["x_w"].rearrange("(m p) n -> p m n", p=P)).then_inc(loaded, 16)
            sp.dma_start(dt_w[:], w["dt_w"]).then_inc(loaded, 16)
            sp.dma_start(out_w[:], w["out_w"].rearrange("(m p) n -> p m n", p=P)).then_inc(loaded, 16)
            sp.dma_start(conv_w[:], w["conv_w"]).then_inc(loaded, 16)
            sp.dma_start(vecs[:], w["vecs"]).then_inc(loaded, 16)
            sp.dma_start(a_cols[:], w["a_log_cols"]).then_inc(loaded, 16)

            def store_bc(c, s):
                sp.wait_ge(work_left, c * ITEMS + X_DBL + 1)
                sp.dma_start(bc_dram[s].rearrange("o n t -> (o n) t"), x_dbl[RANK:RANK + 2 * N_STATE, :]
                             ).then_inc(bc_stored, 16)

            def spread(c, s, n):
                if n == 0:
                    sp.wait_ge(bc_stored, c * 16 + 16)
                if not (isinstance(c, int) and c == 0 and n < BC):
                    sp.wait_ge(v_ready, c * NU + (n - BC + 1) * UPN)
                sp.dma_start(b_rep[:, n % BC], bc_dram[s, 0, n:n + 1, :].broadcast_to([P, CH])
                             ).then_inc(b_loaded[n % BC], 16)
                if not (isinstance(c, int) and c == 0 and n < BC):
                    sp.wait_ge(hc_ready, c * NU + (n - BC + 1) * UPN + HR)
                sp.dma_start(c_rep[:, n % BC], bc_dram[s, 1, n:n + 1, :].broadcast_to([P, CH])
                             ).then_inc(c_loaded[n % BC], 16)

            def chunk(c, s, first, last):
                for n in range(N_STATE):
                    spread(c, s, n)
                    if n == N_STATE - BC and not last:
                        store_bc(c + 1, 1 - s)

            store_bc(0, 0)
            over_chunks(sp, NCH, chunk)

        @block.tensor
        def _(pe):
            def product(c, s, i):
                if i >= 2:
                    pe.wait_ge(work_left, c * ITEMS + i - 1)
                elif isinstance(c, int) and c == 1:
                    pe.wait_ge(work_left, ITEMS)
                    pe.wait_ge(relu_ready, NM)
                elif not (isinstance(c, int) and c == 0):
                    pe.wait_ge(norm.z_ready, (c - 1) * 2 + norm.FREE)
                out = work_ps[(i + s) % 2]
                if i < X_DBL:
                    for half in range(2):
                        last = nc.tensor.matmul(out[:], in_w[:, half, i * P:(i + 1) * P],
                                                xT[:, half, bass.ts(c, CH)],
                                                start=(half == 0), stop=(half == 1))
                elif i == X_DBL:
                    pe.wait_ge(u_ready, c + 1)
                    for m in range(NM):
                        last = nc.tensor.matmul(out[0:RANK + 2 * N_STATE, :], x_w[:, m, :], u[:, s, m, :],
                                                start=(m == 0), stop=(m == NM - 1))
                else:
                    m = i - X_DBL - 1
                    if m == 0:
                        pe.wait_ge(work_left, c * ITEMS + X_DBL + 1)
                    if m >= 2:
                        pe.wait_ge(relu_ready, c * NM + m - 1)
                    last = nc.tensor.matmul(out[:], dt_w[:, m * P:(m + 1) * P], x_dbl[0:RANK, :],
                                            start=True, stop=True)
                last.then_inc(work_ready, 1)

            def add_states(c, q):
                n, pair = q // UPN, q % UPN
                if n == 0:
                    pe.wait_ge(skip_ready, c * NM + (pair + 1) * PAIR)
                pe.wait_ge(hc_ready, c * NU + q + 1 + HR)
                for m in range(PAIR):
                    last = nc.tensor.matmul(y_ps[pair * PAIR + m][:], k["ident"], hc[:, q % HC, m, :],
                                            start=(n == 0), stop=(n == N_STATE - 1))
                last.then_inc(y_ready, 1)

            def project_out(c, s):
                pe.wait_ge(gated, c + 1)
                for half in range(2):
                    for m in range(NM):
                        last = nc.tensor.matmul(work_ps[half][:], out_w[:, m, half * P:(half + 1) * P],
                                                gate[:, s, m, :], start=(m == 0), stop=(m == NM - 1))
                    last.then_inc(out_ready, 1)

            def chunk(c, s, first, last):
                for q in range(NU):
                    if q >= 1:
                        add_states(c, q - 1)
                    elif not first:
                        add_states(c - 1, NU - 1)
                    if q == 4 and not first:
                        pe.wait_ge(work_left, c * ITEMS + ITEMS)
                        pe.wait_ge(relu_ready, c * NM + NM)
                        project_out(c - 1, 1 - s)
                    if q == 6 and not first:
                        norm.mean(pe, c - 1)
                    if q == 12 and not first:
                        norm.variance(pe, c - 1)
                    if not last:
                        if 5 <= q < 5 + 2 * NM:
                            product(c + 1, 1 - s, q - 5)
                        if q == 20:
                            product(c + 1, 1 - s, X_DBL)
                        if 22 <= q < 22 + NM:
                            product(c + 1, 1 - s, q - 21 + X_DBL)

            pe.wait_ge(loaded, LOADS)
            pe.sem_inc(y_ready, HC)
            for i in range(ITEMS):
                product(0, 0, i)
            over_chunks(pe, NCH, chunk)
            add_states(NCH - 1, NU - 1)
            project_out(NCH - 1, 1)
            norm.mean(pe, NCH - 1)
            norm.variance(pe, NCH - 1)

        @block.scalar
        def _(act):
            def leave(c, s, i):
                act.wait_ge(work_ready, c * ITEMS + i + 1)
                src = work_ps[(i + s) % 2]
                if i < NM:
                    if i == 0:
                        act.wait_ge(halo_ready, c + 1)
                    nc.scalar.copy(xin[:, i, HALO:], src[:]).then_inc(work_left, 1)
                    act.wait_ge(work_left, c * ITEMS + i + 1)
                    nc.scalar.activation(u[:, s, i, :], xin[:, i, 0:CH], ACT.Identity,
                                         scale=conv_w[:, i, 0:1], bias=conv_b[:, i:i + 1]
                                         ).then_inc(tap0_ready, 1)
                elif i < X_DBL:
                    nc.scalar.copy(gate[:, s, i - NM, :], src[:]).then_inc(work_left, 1)
                elif i == X_DBL:
                    act.wait_ge(bc_stored, c * 16)
                    nc.scalar.copy(x_dbl[:], src[0:RANK + 2 * N_STATE, :]).then_inc(work_left, 1)
                else:
                    m = i - X_DBL - 1
                    if m == 0:
                        act.wait_ge(log_ready, c)
                        act.wait_ge(dt_ready, c)
                    nc.scalar.activation(dt[:, s, m, :], src[:], ACT.Relu, bias=dt_b[:, m:m + 1]
                                         ).then_inc(relu_ready, 1)
                    nc.scalar.activation(e[:, m, :], src[:], ACT.Abs, bias=dt_b[:, m:m + 1]
                                         ).then_inc(work_left, 1)

            def activate(c, s):
                act.wait_ge(taps_ready, (c + 1) * HALO * NM)
                nc.scalar.activation(u[:, s], u[:, s], ACT.Silu).then_inc(u_ready, 1)
                act.wait_ge(work_left, c * ITEMS + X_DBL)
                nc.scalar.activation(gate[:, s], gate[:, s], ACT.Silu).then_inc(gate_ready, 1)

            def exp_abs(c, s):
                act.wait_ge(work_left, (c + 1) * ITEMS)
                nc.scalar.activation(e[:], e[:], ACT.Exp, scale=-1.0).then_inc(e_ready, 1)
                act.wait_ge(e_ready, c + 1)
                nc.scalar.activation(dtu[:, s], e[:], ACT.Identity, bias=1.0).then_inc(w_ready, 1)

            def log(c, s):
                act.wait_ge(err_ready, c + 1)
                nc.scalar.activation(e[:], e[:], ACT.Ln, bias=1.0).then_inc(ln_ready, 1)

            def chunk(c, s, first, last):
                act.wait_ge(dt_ready, c + 1)
                for q in range(NU):
                    for m in range(PAIR):
                        i = q * PAIR + m
                        act.wait_ge(h_ready, c * NT + i + 1)
                        nc.scalar.activation(decay[:, i % DEC, :], dt[:, s, q % UPN * PAIR + m, :], ACT.Exp,
                                             scale=a_cols[:, i:i + 1]).then_inc(decay_ready, 1)
                    if not last:
                        if 5 <= q < 5 + 2 * NM:
                            leave(c + 1, 1 - s, q - 5)
                        if q == 18:
                            activate(c + 1, 1 - s)
                        if q == 21:
                            leave(c + 1, 1 - s, X_DBL)
                        if 23 <= q < 23 + NM:
                            leave(c + 1, 1 - s, q - 22 + X_DBL)
                        if q == 27:
                            exp_abs(c + 1, 1 - s)
                        if q == 29:
                            log(c + 1, 1 - s)
                    if not first:
                        if q == 9:
                            norm.square(act, c - 1)
                        if q == 15:
                            norm.deviation(act, c - 1)

            act.wait_ge(loaded, LOADS)
            nc.scalar.activation(a_cols[:], a_cols[:], ACT.Exp).then_inc(a_ready, 1)
            act.wait_ge(a_ready, 4)
            for i in range(X_DBL):
                leave(0, 0, i)
            activate(0, 0)
            for i in range(X_DBL, ITEMS):
                leave(0, 0, i)
            exp_abs(0, 0)
            log(0, 0)
            over_chunks(act, NCH, chunk)
            norm.square(act, NCH - 1)
            norm.deviation(act, NCH - 1)

        @block.gpsimd
        def _(pool):
            def weigh_input(c, s):
                pool.wait_ge(dt_ready, c + 1)
                pool.wait_ge(u_ready, c + 1)
                nc.gpsimd.tensor_tensor(dtu[:, s], dt[:, s], u[:, s], ALU.mult).then_inc(dtu_ready, 1)

            def apply_gate(c, s):
                pool.wait_ge(skip_ready, (c + 1) * NM + NM)
                pool.wait_ge(gate_ready, c + 1)
                nc.gpsimd.tensor_tensor(gate[:, s], gate[:, s], u[:, s], ALU.mult).then_inc(gated, 1)

            def chunk(c, s, first, last):
                for q in range(NU):
                    n = q // UPN
                    if q % UPN == 0:
                        pool.wait_ge(c_loaded[n % BC], (c * (N_STATE // BC) + n // BC + 1) * 16)
                    pool.wait_ge(h_ready, c * NT + (q + 1) * PAIR + DEC)
                    pool.wait_ge(y_ready, c * NU + q + 1)
                    nc.gpsimd.tensor_tensor(hc[:, q % HC], h[:, q % HR],
                                            c_rep[:, n % BC].unsqueeze(1).broadcast_to([P, PAIR, CH]),
                                            ALU.mult).then_inc(hc_ready, 1)
                    if q == 2 and not first:
                        apply_gate(c - 1, 1 - s)
                    if q == 30 and not last:
                        weigh_input(c + 1, 1 - s)

            pool.sem_inc(hc_ready, HR)
            weigh_input(0, 0)
            over_chunks(pool, NCH, chunk)
            apply_gate(NCH - 1, 1)

        @block.vector
        def _(dve):
            def tap(c, s, m, j):
                if j == 1:
                    dve.wait_ge(tap0_ready, c * NM + m + 1)
                else:
                    dve.wait_ge(taps_ready, c * HALO * NM + m * HALO + j - 1)
                nc.vector.scalar_tensor_tensor(out=u[:, s, m, :], in0=xin[:, m, j:j + CH],
                                               scalar=conv_w[:, m, j:j + 1], in1=u[:, s, m, :],
                                               op0=ALU.mult, op1=ALU.add).then_inc(taps_ready, 1)

            def keep_halo(c):
                dve.wait_ge(taps_ready, (c + 1) * HALO * NM)
                dve.wait_ge(tap0_ready, (c + 1) * NM)
                nc.vector.tensor_copy(xin[:, :, 0:HALO], xin[:, :, CH:CH + HALO]).then_inc(halo_ready, 1)

            def log_error(c, s):
                dve.wait_ge(w_ready, c + 1)
                nc.vector.scalar_tensor_tensor(out=dtu[:, s], in0=dtu[:, s], scalar=-1.0, in1=e[:],
                                               op0=ALU.add, op1=ALU.subtract).then_inc(err_ready, 1)

            def finish_dt(c, s):
                dve.wait_ge(err_ready, c + 1)
                dve.wait_ge(ln_ready, c + 1)
                nc.vector.tensor_tensor(e[:], e[:], dtu[:, s], ALU.subtract).then_inc(log_ready, 1)
                dve.wait_ge(log_ready, c + 1)
                dve.wait_ge(relu_ready, (c + 1) * NM)
                nc.vector.tensor_tensor(dt[:, s], dt[:, s], e[:], ALU.add).then_inc(dt_ready, 1)

            def spread_input(c, s, q):
                n, pair = q // UPN, q % UPN
                if q == 0:
                    dve.wait_ge(dtu_ready, c + 1)
                if pair == 0:
                    dve.wait_ge(b_loaded[n % BC], (c * (N_STATE // BC) + n // BC + 1) * 16)
                dve.wait_ge(h_ready, c * NT + q * PAIR + DEC - PAIR)
                nc.vector.tensor_tensor(v[:, q % VB], dtu[:, s, pair * PAIR:(pair + 1) * PAIR, :],
                                        b_rep[:, n % BC].unsqueeze(1).broadcast_to([P, PAIR, CH]),
                                        ALU.mult).then_inc(v_ready, 1)

            def scan(c, q):
                dve.wait_ge(v_ready, c * NU + q + 1)
                dve.wait_ge(hc_ready, c * NU + q + 1)
                dve.wait_ge(carry_ready, c * NU + q - HR + 1 + NU)
                for m in range(PAIR):
                    i = q * PAIR + m
                    dve.wait_ge(decay_ready, c * NT + i + 1)
                    nc.vector.tensor_tensor_scan(out=h[:, q % HR, m, :], data0=decay[:, i % DEC, :],
                                                 data1=v[:, q % VB, m, :], initial=carry[:, i:i + 1],
                                                 op0=ALU.mult, op1=ALU.add).then_inc(h_ready, 1)

            def keep_last_states(c, q):
                dve.wait_ge(h_ready, c * NT + (q + 1) * PAIR + DEC)
                nc.vector.tensor_copy(carry[:, q * PAIR:(q + 1) * PAIR], h[:, q % HR, :, CH - 1]
                                      ).then_inc(carry_ready, 1)

            def skip(c, s):
                dve.wait_ge(y_ready, (c + 1) * NU + HC)
                for m in range(NM):
                    nc.vector.scalar_tensor_tensor(out=u[:, s, m, :], in0=u[:, s, m, :],
                                                   scalar=d_skip[:, m:m + 1], in1=y_ps[m][:],
                                                   op0=ALU.mult, op1=ALU.add).then_inc(skip_ready, 1)

            def residual(c):
                for half in range(2):
                    dve.wait_ge(out_ready, c * 2 + half + 1)
                    norm.add_residual(dve, c, half, work_ps[half][:])

            def chunk(c, s, first, last):
                for q in range(NU + 2):
                    if q < NU:
                        spread_input(c, s, q)
                    if 1 <= q <= NU:
                        scan(c, q - 1)
                    if q >= 2:
                        keep_last_states(c, q - 2)
                    if not first:
                        if q == 2:
                            skip(c - 1, 1 - s)
                        if q == 5:
                            residual(c - 1)
                        if q == 7:
                            norm.centre(dve, c - 1)
                        if q == 17:
                            norm.scale(dve, c - 1)
                    if not last:
                        if 8 <= q < 8 + NM * HALO // 2:
                            for t in (2 * (q - 8), 2 * (q - 8) + 1):
                                tap(c + 1, 1 - s, t // HALO, t % HALO + 1)
                        if q == 8 + NM * HALO // 2:
                            keep_halo(c + 1)
                        if q == 28:
                            log_error(c + 1, 1 - s)
                        if q == 31:
                            finish_dt(c + 1, 1 - s)

            dve.wait_ge(a_ready, 1)
            nc.vector.tensor_scalar(a_cols[:], a_cols[:], -1.0, None, ALU.mult).then_inc(a_ready, 1)
            nc.vector.memset(carry[:], 0.0).then_inc(a_ready, 1)
            nc.vector.memset(xin[:, :, 0:HALO], 0.0).then_inc(a_ready, 1)
            dve.wait_ge(a_ready, 4)
            dve.sem_inc(halo_ready, 1)
            dve.sem_inc(h_ready, DEC)
            dve.sem_inc(carry_ready, NU)
            dve.sem_inc(skip_ready, NM)
            dve.sem_inc(norm.z_ready, norm.FREE)
            for m in range(NM):
                for j in range(1, TAPS):
                    tap(0, 0, m, j)
            keep_halo(0)
            log_error(0, 0)
            finish_dt(0, 0)
            over_chunks(dve, NCH, chunk)
            skip(NCH - 1, 1)
            residual(NCH - 1)
            norm.centre(dve, NCH - 1)
            norm.scale(dve, NCH - 1)


def layer1_experts(nc, xT, k, w):
    T = xT.shape[2]
    NCH = T // CH
    BPC = CH // P
    HEADS, DH, E, INNER = 8, 32, w["w1"].shape[1], w["w1"].shape[2]
    assert DH == QUAD and INNER == P and HEADS * DH == 2 * P and HEADS * E == P
    F32R = mybir.dt.float32r
    GROUPS = 2
    HPG = HEADS // GROUPS
    NU = E * GROUPS
    NADD = NU - GROUPS
    HM, UP, EO, PR, WR = 4, 2, 2, 4, 8
    ITEMS = HEADS + 3
    LOGITS, TURN, BACK = HEADS, HEADS + 1, HEADS + 2
    with ExitStack() as ctx:
        def sb(name, shape, dt=F32):
            return ctx.enter_context(nc.sbuf_tensor("d_" + name, shape, dt))

        def sem(name):
            return ctx.enter_context(nc.semaphore("d_" + name))

        up_ps = [ctx.enter_context(nc.psum_tensor(f"d_up{i}", [P, 2, CH], F32)) for i in range(UP)]
        eo_ps = [ctx.enter_context(nc.psum_tensor(f"d_eo{i}", [P, CH], F32)) for i in range(EO)]
        work_ps = ctx.enter_context(nc.psum_tensor("d_work", [P, CH], F32))
        norm_ps = ctx.enter_context(nc.psum_tensor("d_norm", [P, CH], F32))
        w_dram = nc.dram_tensor("d_w_scratch", (2, GROUPS, HPG, E, CH), F32, kind="Internal").ap()
        raw = sb("raw", [P, E * INNER])
        emb_raw = sb("emb_raw", [P, E])
        w1 = sb("w1", [P, E, INNER], F32R)
        emb = sb("emb", [P, HEADS, P], F32R)
        w2 = sb("w2", [P, E, DH])
        b1 = sb("b1", [P, E])
        b2 = sb("b2", [P, E])
        heads_w = sb("heads_w", [P, 2, HEADS, P])
        heads_b = sb("heads_b", [P, HEADS])
        out_w = sb("out_w", [P, 2, 2 * P])
        out_b = sb("out_b", [P, 2])
        order = sb("order", [P, E])
        heads = sb("heads", [P, 2, HEADS, CH], F32R)
        logit = sb("logit", [P, CH])
        probs = sb("probs", [P, BPC * HEADS, E])
        key = sb("key", [P, BPC * HEADS, E])
        mask = sb("mask", [P, BPC * HEADS, E])
        stat = sb("stat", [P, BPC * HEADS])
        w_t = sb("w_t", [P, CH])
        w_rep = sb("w_rep", [P, WR, CH])
        hmid = sb("hmid", [P, HM, 2, CH])
        prod = sb("prod", [P, PR, CH])
        acc = sb("acc", [P, 2, GROUPS, CH])

        loaded = sem("loaded")
        split_ready = sem("split_ready")
        work_ready = sem("work_ready")
        high_ready = sem("high_ready")
        low_ready = sem("low_ready")
        logit_kept = sem("logit_kept")
        route = sem("route")
        picked = sem("picked")
        emb_ready = sem("emb_ready")
        exp_ready = sem("exp_ready")
        wt_ready = sem("wt_ready")
        w_stored = sem("w_stored")
        w_loaded = [sem(f"w_loaded{i}") for i in range(WR)]
        up_ready = sem("up_ready")
        gelu_ready = sem("gelu_ready")
        down_ready = sem("down_ready")
        prod_ready = sem("prod_ready")
        add_ready = sem("add_ready")
        out_ready = sem("out_ready")
        norm = Norm(nc, sb, sem, norm_ps[:], k, xT)
        ROUTE = 11
        NSPLIT = 6

        block = ctx.enter_context(nc.Block())
        LOADS = 10 * 16

        @block.sync
        def _(sp):
            sp.dma_start(raw[:], w["w1"].rearrange("p e i -> p (e i)")).then_inc(loaded, 16)
            sp.dma_start(emb_raw[:], w["emb"]).then_inc(loaded, 16)
            sp.dma_start(w2[:], w["w2"]).then_inc(loaded, 16)
            sp.dma_start(b1[:], w["b1"]).then_inc(loaded, 16)
            sp.dma_start(b2[:], w["b2"]).then_inc(loaded, 16)
            sp.dma_start(heads_w[:], w["heads_w"].rearrange("(h p) g m -> p h g m", p=P)).then_inc(loaded, 16)
            sp.dma_start(heads_b[:], w["heads_b"]).then_inc(loaded, 16)
            sp.dma_start(out_w[:], w["out_w"].rearrange("(h p) m -> p h m", p=P)).then_inc(loaded, 16)
            sp.dma_start(out_b[:], w["out_b"]).then_inc(loaded, 16)
            sp.dma_start(order[:], w["order"]).then_inc(loaded, 16)

            def store_weights(c, s):
                sp.wait_ge(wt_ready, c + 1)
                sp.dma_start(w_dram[s].rearrange("g j e t -> (g j e) t"), w_t[:]).then_inc(w_stored, 16)

            def spread(c, s, q):
                if q == 0:
                    sp.wait_ge(w_stored, c * 16 + 16)
                if not (isinstance(c, int) and c == 0 and q < WR):
                    sp.wait_ge(prod_ready, c * NU + q - WR + 1 + EO)
                src = w_dram[s, q % GROUPS, :, q // GROUPS, :].unsqueeze(1).broadcast_to([HPG, DH, CH])
                sp.dma_start(w_rep[:, q % WR], src).then_inc(w_loaded[q % WR], 16)

            def chunk(c, s, first, last):
                for q in range(NU):
                    spread(c, s, q)
                if not last:
                    store_weights(c + 1, 1 - s)

            store_weights(0, 0)
            over_chunks(sp, NCH, chunk)

        @block.tensor
        def _(pe):
            def product(c, s, i):
                if i <= LOGITS:
                    pe.wait_ge(high_ready, c * HEADS + i)
                    pe.wait_ge(low_ready, c * HEADS + i)
                if i == 0:
                    pe.wait_ge(wt_ready, c)
                if i == 0 and not (isinstance(c, int) and c < 2):
                    pe.wait_ge(norm.z_ready, (c - 1) * 2 + norm.FREE)
                if i < HEADS:
                    for half in range(2):
                        last = nc.tensor.matmul(work_ps[:], heads_w[:, half, i, :], xT[:, half, bass.ts(c, CH)],
                                                start=(half == 0), stop=(half == 1))
                elif i == LOGITS:
                    for g in range(HEADS):
                        last = nc.tensor.matmul(work_ps[:], emb[:, g, :], heads[:, s, g, :],
                                                start=(g == 0), stop=(g == HEADS - 1))
                elif i == TURN:
                    pe.wait_ge(logit_kept, c + 1)
                    for b in range(BPC):
                        last = nc.tensor.transpose(work_ps[:, b * P:(b + 1) * P], logit[:, b * P:(b + 1) * P],
                                                   k["ident"])
                else:
                    pe.wait_ge(route, (c + 1) * ROUTE)
                    for b in range(BPC):
                        last = nc.tensor.transpose(
                            work_ps[:, b * P:(b + 1) * P],
                            probs[:, b * HEADS:(b + 1) * HEADS, :].rearrange("p g e -> p (g e)"), k["ident"])
                last.then_inc(work_ready, 1)

            def up(c, s, q, r):
                e, g = q // GROUPS, q % GROUPS
                if q == 0 and r == 0:
                    pe.wait_ge(low_ready, (c + 1) * HEADS)
                    pe.wait_ge(high_ready, (c + 1) * HEADS)
                pe.wait_ge(gelu_ready, c * 2 * NU + 2 * q + r + 1)
                for j in range(2):
                    last = nc.tensor.matmul(up_ps[r][:, j, :], w1[:, e, :], heads[:, s, g * HPG + 2 * r + j, :],
                                            start=True, stop=True)
                last.then_inc(up_ready, 1)

            def down(c, q):
                e = q // GROUPS
                pe.wait_ge(gelu_ready, c * 2 * NU + 2 * q + 2 + UP)
                pe.wait_ge(prod_ready, c * NU + q + 1)
                for j in range(HPG):
                    last = nc.tensor.matmul(eo_ps[q % EO][j * DH:(j + 1) * DH, :], w2[:, e, :],
                                            hmid[:, (2 * q + j // 2) % HM, j % 2, :], start=True, stop=True)
                last.then_inc(down_ready, 1)

            def project_out(c, s, half):
                if half == 0:
                    pe.wait_ge(add_ready, (c + 1) * NADD)
                    pe.wait_ge(wt_ready, NCH if isinstance(c, int) and c == NCH - 1 else c + 2)
                else:
                    pe.wait_ge(norm.z_ready, c * 2 + 1 + norm.FREE)
                for g in range(GROUPS):
                    last = nc.tensor.matmul(work_ps[:], out_w[:, g, half * P:(half + 1) * P], acc[:, s, g, :],
                                            start=(g == 0), stop=(g == GROUPS - 1))
                last.then_inc(out_ready, 1)

            def chunk(c, s, first, last):
                for q in range(NU):
                    up(c, s, q, 0)
                    up(c, s, q, 1)
                    if q >= 1:
                        down(c, q - 1)
                    elif not first:
                        down(c - 1, NU - 1)
                    if not first:
                        if q in (3, 5):
                            project_out(c - 1, 1 - s, (q - 3) // 2)
                        if q == 7:
                            norm.mean(pe, c - 1)
                        if q == 11:
                            norm.variance(pe, c - 1)
                    if not last:
                        if 7 <= q < 7 + 2 * HEADS and q % 2 == 1:
                            product(c + 1, 1 - s, (q - 7) // 2)
                        if q == 22:
                            product(c + 1, 1 - s, LOGITS)
                        if q == 24:
                            product(c + 1, 1 - s, TURN)
                        if q == 30:
                            product(c + 1, 1 - s, BACK)

            pe.wait_ge(split_ready, NSPLIT)
            pe.wait_ge(emb_ready, 3 * HEADS)
            pe.sem_inc(down_ready, HM // 2)
            for i in range(ITEMS):
                product(0, 0, i)
            over_chunks(pe, NCH, chunk)
            down(NCH - 1, NU - 1)
            project_out(NCH - 1, 1, 0)
            project_out(NCH - 1, 1, 1)
            norm.mean(pe, NCH - 1)
            norm.variance(pe, NCH - 1)

        @block.scalar
        def _(act):
            def high(c, s, i):
                act.wait_ge(work_ready, c * ITEMS + i + 1)
                nc.scalar.activation(heads[:, s, i, :], work_ps[:], ACT.Identity, bias=heads_b[:, i:i + 1]
                                     ).then_inc(high_ready, 1)

            def keep_logits(c):
                act.wait_ge(work_ready, c * ITEMS + LOGITS + 1)
                nc.scalar.copy(logit[:], work_ps[:]).then_inc(logit_kept, 1)

            def exp(c):
                act.wait_ge(route, c * ROUTE + 2)
                nc.scalar.activation(probs[:], probs[:], ACT.Exp).then_inc(exp_ready, 1)

            def keep_weights(c):
                act.wait_ge(work_ready, (c + 1) * ITEMS)
                act.wait_ge(w_stored, c * 16)
                nc.scalar.copy(w_t[:], work_ps[:]).then_inc(wt_ready, 1)

            def chunk(c, s, first, last):
                for q in range(NU):
                    e = q // GROUPS
                    for r in range(2):
                        act.wait_ge(up_ready, c * 2 * NU + 2 * q + r + 1)
                        if r == 0:
                            act.wait_ge(down_ready, c * NU + q + 1)
                        nc.scalar.activation(hmid[:, (2 * q + r) % HM], up_ps[r][:], ACT.Gelu,
                                             bias=b1[:, e:e + 1]).then_inc(gelu_ready, 1)
                    if not last:
                        if 7 <= q < 7 + 2 * HEADS and q % 2 == 1:
                            high(c + 1, 1 - s, (q - 7) // 2)
                        if q == 22:
                            keep_logits(c + 1)
                        if q == 26:
                            exp(c + 1)
                        if q == 31:
                            keep_weights(c + 1)
                    if not first:
                        if q == 9:
                            norm.square(act, c - 1)
                        if q == 12:
                            norm.deviation(act, c - 1)

            act.wait_ge(split_ready, NSPLIT)
            act.sem_inc(gelu_ready, UP)
            for i in range(HEADS):
                high(0, 0, i)
            keep_logits(0)
            exp(0)
            keep_weights(0)
            over_chunks(act, NCH, chunk)
            norm.square(act, NCH - 1)
            norm.deviation(act, NCH - 1)

        @block.gpsimd
        def _(pool):
            def chunk(c, s, first, last):
                for q in range(GROUPS, NU):
                    g = q % GROUPS
                    pool.wait_ge(prod_ready, c * NU + q + 1 + EO)
                    if q >= 2 * GROUPS:
                        pool.wait_ge(add_ready, c * NADD + q - 2 * GROUPS + 1)
                    nc.gpsimd.tensor_tensor(acc[:, s, g, :], acc[:, s, g, :], prod[:, q % PR, :], ALU.add
                                            ).then_inc(add_ready, 1)

            over_chunks(pool, NCH, chunk)

        @block.vector
        def _(dve):
            def low(c, s, i):
                rows = slice(2 * DH, 4 * DH)
                dve.wait_ge(high_ready, c * HEADS + i + 1)
                nc.vector.scalar_tensor_tensor(out=heads[rows, s, i, :], in0=work_ps[rows, :],
                                               scalar=heads_b[rows, i:i + 1],
                                               in1=heads[rows, s, i, :].bitcast(F32),
                                               op0=ALU.add, op1=ALU.subtract).then_inc(low_ready, 1)

            def per_head(a):
                return a.unsqueeze(2).broadcast_to([P, BPC * HEADS, E])

            def step(c, n, ins):
                ins.then_inc(route, 1)
                dve.wait_ge(route, c * ROUTE + n)

            def route_max(c):
                dve.wait_ge(work_ready, c * ITEMS + TURN + 1)
                turned = work_ps[:].rearrange("p (g e) -> p g e", e=E)
                step(c, 1, nc.vector.reduce_max(stat[:], turned, axis=AX_X))
                step(c, 2, nc.vector.tensor_tensor(probs[:], turned, per_head(stat[:]), ALU.subtract))

            def route_pick(c):
                dve.wait_ge(exp_ready, c + 1)
                step(c, 3, nc.vector.reduce_sum(stat[:], probs[:], axis=AX_X))
                step(c, 4, nc.vector.reciprocal(stat[:], stat[:]))
                step(c, 5, nc.vector.tensor_tensor(probs[:], probs[:], per_head(stat[:]), ALU.mult))
                step(c, 6, nc.vector.tensor_tensor(
                    key[:], probs[:], order[:].unsqueeze(1).broadcast_to([P, BPC * HEADS, E]), ALU.mult))
                step(c, 7, nc.vector.reduce_max(stat[:], key[:], axis=AX_X))
                step(c, 8, nc.vector.tensor_tensor(mask[:], key[:], per_head(stat[:]), ALU.is_lt))
                step(c, 9, nc.vector.tensor_tensor(mask[:], mask[:], key[:], ALU.mult))
                step(c, 10, nc.vector.reduce_max(stat[:], mask[:], axis=AX_X))
                nc.vector.tensor_tensor(mask[:], key[:], per_head(stat[:]), ALU.is_ge).then_inc(picked, 1)
                dve.wait_ge(picked, c + 1)
                step(c, 11, nc.vector.tensor_tensor(probs[:], probs[:], mask[:], ALU.mult))

            def weigh(c, s, q):
                e, g = q // GROUPS, q % GROUPS
                dve.wait_ge(w_loaded[q % WR], (c * (NU // WR) + q // WR + 1) * 16)
                dve.wait_ge(down_ready, c * NU + q + 1 + HM // 2)
                if q < GROUPS:
                    out = acc[:, s, g, :]
                else:
                    dve.wait_ge(add_ready, c * NADD + max(q - PR - GROUPS + 1, 0))
                    out = prod[:, q % PR, :]
                nc.vector.scalar_tensor_tensor(out=out, in0=eo_ps[q % EO][:], scalar=b2[:, e:e + 1],
                                               in1=w_rep[:, q % WR, :], op0=ALU.add, op1=ALU.mult
                                               ).then_inc(prod_ready, 1)

            def residual(c, half):
                dve.wait_ge(out_ready, c * 2 + half + 1)
                norm.add_residual(dve, c, half, work_ps[:], out_b[:, half:half + 1])

            def chunk(c, s, first, last):
                for q in range(NU + 1):
                    if q >= 1:
                        weigh(c, s, q - 1)
                    if not first:
                        if q in (4, 6):
                            residual(c - 1, (q - 4) // 2)
                        if q == 8:
                            norm.centre(dve, c - 1)
                        if q == 14:
                            norm.scale(dve, c - 1)
                    if not last:
                        if 8 <= q < 8 + 2 * HEADS and q % 2 == 0:
                            low(c + 1, 1 - s, (q - 8) // 2)
                        if q == 25:
                            route_max(c + 1)
                        if q == 28:
                            route_pick(c + 1)

            dve.wait_ge(loaded, LOADS)
            nc.vector.memset(emb[:].bitcast(F32), 0.0).then_inc(split_ready, 1)
            nc.vector.tensor_copy(w1[:], raw[:].rearrange("p (e i) -> p e i", e=E)).then_inc(split_ready, 1)
            dve.wait_ge(split_ready, 2)
            for g in range(HEADS):
                nc.vector.tensor_copy(emb[:, g, g * E:(g + 1) * E], emb_raw[:]).then_inc(emb_ready, 1)
            dve.wait_ge(emb_ready, HEADS)
            for i in (1, 3):
                rows = slice(i * DH, (i + 1) * DH)
                nc.vector.tensor_tensor(w1[rows], raw[rows].rearrange("p (e i) -> p e i", e=E),
                                        w1[rows].bitcast(F32), ALU.subtract).then_inc(split_ready, 1)
                nc.vector.tensor_tensor(emb_raw[rows], emb_raw[rows], emb[rows, 0, 0:E].bitcast(F32),
                                        ALU.subtract).then_inc(split_ready, 1)
            dve.wait_ge(split_ready, NSPLIT)
            for i in (1, 3):
                rows = slice(i * DH, (i + 1) * DH)
                for g in range(HEADS):
                    nc.vector.tensor_copy(emb[rows, g, g * E:(g + 1) * E], emb_raw[rows]).then_inc(emb_ready, 1)
            dve.wait_ge(emb_ready, 3 * HEADS)
            dve.sem_inc(prod_ready, EO)
            dve.sem_inc(norm.z_ready, norm.FREE)
            for i in range(HEADS):
                low(0, 0, i)
            route_max(0)
            route_pick(0)
            over_chunks(dve, NCH, chunk)
            residual(NCH - 1, 0)
            residual(NCH - 1, 1)
            norm.centre(dve, NCH - 1)
            norm.scale(dve, NCH - 1)


def build(nc, d, T):
    with ExitStack() as ctx:
        def sb(name, shape):
            return ctx.enter_context(nc.sbuf_tensor(name, shape, F32))

        xT = sb("xT", [P, 2, T])
        sel_rep = sb("sel_rep", [P, KPQ, P])
        sel_sum = sb("sel_sum", [P, KPQ, QUAD])
        avg = sb("avg", [P, P])
        eps = sb("eps", [P, 1])
        ident = sb("ident", [P, P])
        loaded = ctx.enter_context(nc.semaphore("x_loaded"))
        stored = ctx.enter_context(nc.semaphore("x_stored"))
        k = {"sel_rep": sel_rep, "sel_sum": sel_sum, "avg": avg[:], "eps": eps[:], "ident": ident[:]}
        with nc.Block() as block:
            @block.vector
            def _(dve):
                nc.vector.memset(eps[:], EPS)

            @block.sync
            def _(sp):
                sp.dma_start(xT[:], d["xT"].rearrange("(h p) t -> p h t", p=P)).then_inc(loaded, 16)
                sp.dma_start(sel_rep[:], d["sel_rep"]).then_inc(loaded, 16)
                sp.dma_start(sel_sum[:], d["sel_sum"]).then_inc(loaded, 16)
                sp.dma_start(avg[:], d["avg"]).then_inc(loaded, 16)
                sp.dma_start(ident[:], d["ident"]).then_inc(loaded, 16)
                sp.wait_ge(loaded, 80)
        layer0_scan(nc, xT, k, {n[2:]: a for n, a in d.items() if n.startswith("a_")})
        layer0_experts(nc, xT, k, {n[2:]: a for n, a in d.items() if n.startswith("b_")})
        layer1_scan(nc, xT, k, {n[2:]: a for n, a in d.items() if n.startswith("c_")})
        layer1_experts(nc, xT, k, {n[2:]: a for n, a in d.items() if n.startswith("d_")})
        with nc.Block() as block:
            @block.sync
            def _(sp):
                sp.dma_start(d["out"].rearrange("(h p) t -> p h t", p=P), xT[:]).then_inc(stored, 16)
                sp.wait_ge(stored, 16)


def kernel(**inputs):
    import numpy as np
    import concourse.bacc as bacc
    from concourse.bass_utils import run_bass_kernel_spmd

    D = inputs["L0_attn_sequence"].shape[2]
    T = inputs["L0_attn_sequence"].shape[1]
    x = {n: np.asarray(a) for n, a in inputs.items()}

    def scan_cols(a):
        return a.reshape(-1, NQ, KPQ, P).transpose(3, 0, 2, 1).reshape(P, -1)

    def cols(a):
        return a.reshape(-1, P).T

    row = np.arange(P)
    sel_rep = np.zeros((P, KPQ, P), np.float32)
    sel_sum = np.zeros((P, KPQ, QUAD), np.float32)
    for kk in range(KPQ):
        sel_rep[:, kk, :] = (row[:, None] % QUAD) == (row[None, :] // N_STATE + DPT * kk)
        sel_sum[:, kk, :] = (row[:, None] // N_STATE + DPT * kk) == np.arange(QUAD)[None, :]
    w_bc = np.stack([np.tile(x["L0_attn_W_B"].T, (1, DPT)), np.tile(x["L0_attn_W_C"].T, (1, DPT)),
                     np.tile(x["L0_attn_W_Delta"].T, (1, P))], axis=1)
    def with_shared(name):
        return np.concatenate([x["L0_ffn_" + name], x["L0_ffn_" + name + "_s"][None]])

    def halves(a):
        return a.reshape(a.shape[0], 2, P, a.shape[2]).transpose(0, 2, 1, 3).reshape(a.shape[0], P, -1)

    experts = np.concatenate([halves(with_shared("Wg")), halves(with_shared("Wu")), with_shared("Wd"),
                              with_shared("bg")[:, :, None], with_shared("bu")[:, :, None]], axis=2)
    arrays = {
        "xT": x["L0_attn_sequence"][0].T,
        "sel_rep": sel_rep, "sel_sum": sel_sum, "avg": np.full((P, P), 1.0 / D, np.float32),
        "ident": np.eye(P, dtype=np.float32),
        "a_w_bc": w_bc, "a_x": x["L0_attn_sequence"][0].T,
        "a_b_b": np.tile(x["L0_attn_b_B"], DPT)[:, None], "a_b_c": np.tile(x["L0_attn_b_C"], DPT)[:, None],
        "a_b_step": np.tile(x["L0_attn_b_Delta"], P)[:, None],
        "a_bias_step": np.tile(x["L0_attn_bias_Delta"], P)[:, None],
        "a_a_cols": scan_cols(x["L0_attn_A"]),
        "b_router_w": x["L0_ffn_Wr"], "b_router_b": x["L0_ffn_br"][:, None],
        "b_down_b": np.concatenate([x["L0_ffn_bd"], x["L0_ffn_bd_s"][None]]),
        "b_experts": experts,
        "c_in_w": x["L1_attn_in_proj_w"].T, "c_x_w": x["L1_attn_x_proj_w"].T,
        "c_dt_w": x["L1_attn_dt_proj_w"].T, "c_out_w": x["L1_attn_out_proj_w"].T,
        "c_conv_w": x["L1_attn_conv_w"].reshape(-1, P, x["L1_attn_conv_w"].shape[1]).transpose(1, 0, 2),
        "c_vecs": np.stack([cols(x["L1_attn_conv_b"]), cols(x["L1_attn_dt_proj_b"]),
                            cols(x["L1_attn_D_param"])], axis=1),
        "d_w1": np.tile(x["L1_ffn_W1"].transpose(1, 0, 2), (4, 1, 1)),
        "d_emb": np.tile(x["L1_ffn_expert_emb"], (4, 1)),
        "d_w2": x["L1_ffn_W2"].transpose(1, 0, 2), "d_b1": x["L1_ffn_b1"].T,
        "d_b2": np.tile(x["L1_ffn_b2"].T, (4, 1)),
        "d_heads_w": np.tile(x["L1_ffn_Wm"].reshape(D, -1, 1, QUAD), (1, 1, NQ, 1)).reshape(D, -1, P),
        "d_heads_b": np.tile(x["L1_ffn_bm"].reshape(-1, QUAD).T, (NQ, 1)),
        "d_out_w": x["L1_ffn_Wo"], "d_out_b": cols(x["L1_ffn_bo"]),
        "d_order": np.tile((1.0 + np.arange(15, -1, -1) * 2.0**-22).astype(np.float32), (P, 1)),
        "c_a_log_cols": x["L1_attn_A_log"].reshape(-1, P, N_STATE).transpose(1, 2, 0).reshape(P, -1),
    }
    nc = bacc.Bacc("TRN2", target_bir_lowering=False, num_devices=1)
    arrays = {n: np.ascontiguousarray(a) for n, a in arrays.items()}
    d = {n: nc.dram_tensor("in_" + n, a.shape, mybir.dt.from_np(a.dtype), kind="ExternalInput").ap()
         for n, a in arrays.items()}
    d["out"] = nc.dram_tensor("out_0", (D, T), F32, kind="ExternalOutput").ap()
    build(nc, d, T)
    r = run_bass_kernel_spmd(nc, [{"in_" + n: a for n, a in arrays.items()}], core_ids=[0])
    return np.ascontiguousarray(r.results[0]["out_0"].T)[None]
```

```python
from contextlib import ExitStack

import concourse.bass as bass
from concourse import mybir

ALU = mybir.AluOpType
ACT = mybir.ActivationFunctionType
F32 = mybir.dt.float32
AX_X = mybir.AxisListType.X

P = 128
CH = 512
N_STATE = 16
DPT = P // N_STATE
QUAD = 32
NQ = P // QUAD
KPQ = QUAD // DPT
TPB = NQ * KPQ
EPS = 1e-5


class Norm:

    FREE = 2

    def __init__(self, nc, sb, sem, bank, k, xT):
        self.nc, self.avg, self.eps, self.xT = nc, k["avg"], k["eps"], xT
        self.mean_ps = self.var_ps = bank
        self.z, self.zc, self.rstd = sb("norm_z", [P, 2, CH]), sb("norm_zc", [P, 2, CH]), sb("norm_rstd", [P, CH])
        self.sq = self.z
        self.z_ready = sem("norm_z_ready")
        self.mean_ready = sem("norm_mean_ready")
        self.zc_ready = sem("norm_zc_ready")
        self.sq_ready = sem("norm_sq_ready")
        self.var_ready = sem("norm_var_ready")
        self.log_ready = sem("norm_log_ready")
        self.rstd_ready = sem("norm_rstd_ready")
        self.x_ready = sem("norm_x_ready")

    def add_residual(self, dve, c, half, out_ps, bias=0.0):
        dve.wait_ge(self.var_ready, c)
        self.nc.vector.scalar_tensor_tensor(out=self.z[:, half], in0=out_ps, scalar=bias,
                                            in1=self.xT[:, half, bass.ts(c, CH)], op0=ALU.add,
                                            op1=ALU.add).then_inc(self.z_ready, 1)

    def mean(self, pe, c):
        pe.wait_ge(self.z_ready, c * 2 + 2 + self.FREE)
        pe.wait_ge(self.log_ready, c)
        self.nc.tensor.matmul(self.mean_ps, self.avg, self.z[:, 0], start=True, stop=False)
        self.nc.tensor.matmul(self.mean_ps, self.avg, self.z[:, 1], start=False,
                              stop=True).then_inc(self.mean_ready, 1)

    def centre(self, dve, c):
        dve.wait_ge(self.mean_ready, c + 1)
        dve.wait_ge(self.x_ready, c * 2)
        for half in range(2):
            self.nc.vector.tensor_tensor(self.zc[:, half], self.z[:, half], self.mean_ps,
                                         ALU.subtract).then_inc(self.zc_ready, 1)

    def square(self, act, c):
        act.wait_ge(self.zc_ready, c * 2 + 2)
        self.nc.scalar.activation(self.sq[:], self.zc[:], ACT.Square).then_inc(self.sq_ready, 1)

    def variance(self, pe, c):
        pe.wait_ge(self.sq_ready, c + 1)
        self.nc.tensor.matmul(self.var_ps, self.avg, self.sq[:, 0], start=True, stop=False)
        self.nc.tensor.matmul(self.var_ps, self.avg, self.sq[:, 1], start=False,
                              stop=True).then_inc(self.var_ready, 1)

    def deviation(self, act, c):
        act.wait_ge(self.var_ready, c + 1)
        act.wait_ge(self.x_ready, c * 2)
        self.nc.scalar.activation(self.rstd[:], self.var_ps, ACT.Ln,
                                  bias=self.eps).then_inc(self.log_ready, 1)
        act.wait_ge(self.log_ready, c + 1)
        self.nc.scalar.activation(self.rstd[:], self.rstd[:], ACT.Exp, scale=-0.5).then_inc(self.rstd_ready, 1)

    def scale(self, dve, c):
        dve.wait_ge(self.rstd_ready, c + 1)
        self.scale_now(self.nc.vector, c)

    def scale_now(self, ops, c):
        for half in range(2):
            ops.tensor_tensor(self.xT[:, half, bass.ts(c, CH)], self.zc[:, half], self.rstd[:], ALU.mult
                              ).then_inc(self.x_ready, 1)


def over_chunks(eng, n_chunks, chunk):
    chunk(0, 0, first=True, last=False)
    if n_chunks > 2:
        chunk(1, 1, first=False, last=False)
        if n_chunks > 4:
            with eng.Fori(1, n_chunks // 2 - 1) as i:
                chunk(i * 2, 0, first=False, last=False)
                chunk(i * 2 + 1, 1, first=False, last=False)
        chunk(n_chunks - 2, 0, first=False, last=False)
    chunk(n_chunks - 1, 1, first=False, last=True)


def layer0_scan(nc, xT, k, w):
    T = xT.shape[2]
    NCH = T // CH
    NT = 2 * TPB
    REP, AB, VB, BB, HR, HC = 4, 4, 2, 2, 8, 16
    LAG = 2 * NQ
    Q_RES, Q_MEAN, Q_CENTRE, Q_SQUARE, Q_VAR, Q_SCALE = 7, 8, 10, 14, 16, 22
    Q_PROJ, Q_B, Q_STEP, Q_FINISH, Q_HIGH, Q_LOW = 7, 9, 20, 22, 4, 4
    with ExitStack() as ctx:
        def sb(name, shape, dt=F32):
            return ctx.enter_context(nc.sbuf_tensor("a_" + name, shape, dt))

        def sem(name):
            return ctx.enter_context(nc.semaphore("a_" + name))

        ps = [ctx.enter_context(nc.psum_tensor(f"a_ps{i}", [P, CH], F32)) for i in range(8)]
        rep_ps, y_ps, proj_ps, norm_ps = ps[0:REP], ps[4:6], ps[6], ps[7]
        w_bc = sb("w_bc", [P, 2, 3, P])
        bias = sb("bias", [P, 4])
        step_bias = sb("step_bias", [P, 1])
        a_cols = sb("a_cols", [P, NT])
        inv_a = sb("inv_a", [P, NT])
        x_c = sb("x_c", [P, 2, 2, CH])
        x_parts = [sb(f"x_{n}", [P, 2, 2, CH], mybir.dt.float32r) for n in ("high", "low")]
        sel_rep = sb("sel_rep", [P, KPQ, P], mybir.dt.float32r)
        b_rep = sb("b_rep", [P, 2, CH])
        c_rep = sb("c_rep", [P, 2, CH])
        step = sb("step", [P, 2, CH])
        absz = sb("absz", [P, CH])
        e = sb("e", [P, CH])
        err = sb("err", [P, CH])
        ln = sb("ln", [P, CH])
        relu = sb("relu", [P, CH])
        decay = sb("decay", [P, AB, CH])
        v = sb("v", [P, VB, CH])
        drive = sb("drive", [P, BB, CH])
        h = sb("h", [P, HR, CH])
        carry = sb("carry", [P, NT])
        hc = sb("hc", [P, HC, CH])

        loaded = sem("loaded")
        xc_loaded = [sem("xc_loaded0"), sem("xc_loaded1")]
        const_ready = sem("const_ready")
        x_high = sem("x_high")
        x_low = sem("x_low")
        proj_ready = sem("proj_ready")
        proj_left = sem("proj_left")
        b_ready = sem("b_ready")
        c_ready = sem("c_ready")
        abs_ready = sem("abs_ready")
        e_ready = sem("e_ready")
        ln_ready = sem("ln_ready")
        round_ready = sem("round_ready")
        err_ready = sem("err_ready")
        log_ready = sem("log_ready")
        step_ready = sem("step_ready")
        rep_ready = sem("rep_ready")
        decay_ready = sem("decay_ready")
        v_ready = sem("v_ready")
        drive_ready = sem("drive_ready")
        h_ready = sem("h_ready")
        carry_ready = sem("carry_ready")
        hc_ready = sem("hc_ready")
        y_ready = sem("y_ready")
        norm = Norm(nc, sb, sem, norm_ps[:], k, xT)

        block = ctx.enter_context(nc.Block())
        LOADS = 6 * 16

        @block.sync
        def _(sp):
            sp.dma_start(w_bc[:], w["w_bc"].rearrange("(h p) c m -> p h c m", p=P)).then_inc(loaded, 16)
            sp.dma_start(bias[:, 0:1], w["b_b"]).then_inc(loaded, 16)
            sp.dma_start(bias[:, 1:2], w["b_c"]).then_inc(loaded, 16)
            sp.dma_start(bias[:, 2:3], w["b_step"]).then_inc(loaded, 16)
            sp.dma_start(bias[:, 3:4], w["bias_step"]).then_inc(loaded, 16)
            sp.dma_start(a_cols[:], w["a_cols"]).then_inc(loaded, 16)

            def chunk(c, s, first, last):
                if not (first or (isinstance(c, int) and c == 1)):
                    sp.wait_ge(x_low, c - 1)
                sp.dma_start(x_c[:, s], w["x"].rearrange("(h p) t -> p h t", p=P)[:, :, bass.ts(c, CH)]
                             ).then_inc(xc_loaded[s], 16)

            over_chunks(sp, NCH, chunk)

        @block.tensor
        def _(pe):
            def project(c, i):
                if isinstance(c, int) and c == 2:
                    pe.wait_ge(k["rest_loaded"], 16)
                pe.wait_ge(proj_left, c * 3 + i)
                for half in range(2):
                    last = nc.tensor.matmul(proj_ps[:], w_bc[:, half, i, :], xT[:, half, bass.ts(c, CH)],
                                            start=(half == 0), stop=(half == 1))
                last.then_inc(proj_ready, 1)

            def replicate(c, s, n):
                m, kk, j = n // TPB, n % TPB // NQ, n % NQ
                if n == 0:
                    pe.wait_ge(x_high, c + 1)
                    pe.wait_ge(x_low, c + 1)
                pe.wait_ge(v_ready, c * NT + n + 1)
                q = slice(QUAD * j, QUAD * j + QUAD)
                nc.tensor.matmul(rep_ps[n % REP][:], sel_rep[q, kk, :], x_parts[0][q, s, m, :],
                                 start=True, stop=False)
                nc.tensor.matmul(rep_ps[n % REP][:], sel_rep[q, kk, :], x_parts[1][q, s, m, :],
                                 start=False, stop=True).then_inc(rep_ready, 1)

            def add_states(c, n):
                m, kk, j = n // TPB, n % TPB // NQ, n % NQ
                if n % TPB == 0:
                    pe.wait_ge(norm.z_ready, c * 2 + m + 1)
                pe.wait_ge(hc_ready, c * NT + n + 1 + HR)
                nc.tensor.matmul(y_ps[m][QUAD * j:QUAD * j + QUAD, :], k["sel_sum"][:, kk, :],
                                 hc[:, n % HC, :], start=(kk == 0), stop=(kk == KPQ - 1)
                                 ).then_inc(y_ready, 1)

            def chunk(c, s, first, last):
                for g in range(0, NT, NQ):
                    for n in range(g, g + NQ):
                        replicate(c, s, n)
                    for n in range(g - LAG, g - LAG + NQ):
                        if n >= 0:
                            add_states(c, n)
                        elif not first:
                            add_states(c - 1, NT + n)
                    if g // NQ == Q_MEAN // NQ and not first:
                        norm.mean(pe, c - 1)
                    if g // NQ == Q_VAR // NQ and not first:
                        norm.variance(pe, c - 1)
                    if 0 <= g // NQ - Q_PROJ // NQ < 3 and not last:
                        project(c + 1, g // NQ - Q_PROJ // NQ)

            pe.wait_ge(loaded, LOADS)
            pe.wait_ge(const_ready, 4)
            pe.sem_inc(y_ready, HC)
            for i in range(3):
                project(0, i)
            over_chunks(pe, NCH, chunk)
            for n in range(NT - LAG, NT):
                add_states(NCH - 1, n)
            norm.mean(pe, NCH - 1)
            norm.variance(pe, NCH - 1)

        @block.scalar
        def _(act):
            def spread(c, s, i):
                act.wait_ge(proj_ready, c * 3 + i + 1)
                if i < 2:
                    dst, done = ((b_rep, b_ready), (c_rep, c_ready))[i]
                    nc.scalar.activation(dst[:, s, :], proj_ps[:], ACT.Identity,
                                         bias=bias[:, i:i + 1]).then_inc(done, 1)
                    act.wait_ge(done, c + 1)
                    act.sem_inc(proj_left, 1)
                else:
                    act.wait_ge(step_ready, c)
                    nc.scalar.activation(relu[:], proj_ps[:], ACT.Relu, bias=step_bias[:]
                                         ).then_inc(abs_ready, 1)
                    nc.scalar.activation(absz[:], proj_ps[:], ACT.Abs, bias=step_bias[:]
                                         ).then_inc(abs_ready, 1)
                    act.wait_ge(abs_ready, c * 2 + 2)
                    act.sem_inc(proj_left, 1)
                    nc.scalar.activation(e[:], absz[:], ACT.Exp, scale=-1.0).then_inc(e_ready, 1)
                    act.wait_ge(e_ready, c + 1)
                    nc.scalar.activation(ln[:], e[:], ACT.Ln, bias=1.0).then_inc(ln_ready, 1)
                    nc.scalar.activation(err[:], e[:], ACT.Identity, bias=1.0).then_inc(round_ready, 1)
                    act.wait_ge(round_ready, c * 2 + 1)
                    nc.scalar.activation(err[:], err[:], ACT.Identity, bias=-1.0).then_inc(round_ready, 1)

            def high(c, s):
                act.wait_ge(xc_loaded[s], (c - s) * 8 + 16)
                if not (isinstance(c, int) and c < 2):
                    act.wait_ge(rep_ready, (c - 1) * NT)
                nc.scalar.copy(x_parts[0][:, s], x_c[:, s]).then_inc(x_high, 1)

            def chunk(c, s, first, last):
                act.wait_ge(step_ready, c + 1)
                for n in range(NT):
                    act.wait_ge(h_ready, c * NT + n + 1)
                    nc.scalar.activation(decay[:, n % AB, :], step[:, s, :], ACT.Exp,
                                         scale=a_cols[:, n:n + 1]).then_inc(decay_ready, 1)
                    if n in (Q_B, Q_B + NQ, Q_STEP) and not last:
                        if n == Q_B:
                            act.wait_ge(hc_ready, c * NT + HR)
                        spread(c + 1, 1 - s, 2 if n == Q_STEP else (n - Q_B) // NQ)
                    if n == Q_HIGH and not last:
                        high(c + 1, 1 - s)
                    if n == Q_SQUARE and not first:
                        norm.square(act, c - 1)
                    if n == Q_STEP and not first:
                        norm.deviation(act, c - 1)

            act.wait_ge(const_ready, 4)
            high(0, 0)
            for i in range(3):
                spread(0, 0, i)
            over_chunks(act, NCH, chunk)
            norm.square(act, NCH - 1)
            norm.deviation(act, NCH - 1)

        @block.gpsimd
        def _(pool):
            def finish_step(c, s):
                pool.wait_ge(round_ready, c * 2 + 2)
                nc.gpsimd.tensor_tensor(err[:], e[:], err[:], ALU.subtract).then_inc(err_ready, 1)
                pool.wait_ge(err_ready, c + 1)
                pool.wait_ge(ln_ready, c + 1)
                nc.gpsimd.tensor_tensor(ln[:], ln[:], err[:], ALU.add).then_inc(log_ready, 1)
                pool.wait_ge(log_ready, c + 1)
                nc.gpsimd.tensor_tensor(step[:, s, :], ln[:], relu[:], ALU.add).then_inc(step_ready, 1)

            def low(c, s):
                pool.wait_ge(x_high, c + 1)
                nc.gpsimd.tensor_tensor(x_parts[1][:, s], x_c[:, s], x_parts[0][:, s].bitcast(F32), ALU.subtract
                                        ).then_inc(x_low, 1)

            def chunk(c, s, first, last):
                pool.wait_ge(c_ready, c + 1)
                for n in range(NT):
                    if n == Q_SCALE and not first:
                        pool.wait_ge(norm.rstd_ready, c)
                    pool.wait_ge(h_ready, c * NT + n + 1 + AB)
                    pool.wait_ge(y_ready, c * NT + n + 1)
                    nc.gpsimd.tensor_tensor(hc[:, n % HC, :], h[:, n % HR, :], c_rep[:, s, :],
                                            ALU.mult).then_inc(hc_ready, 1)
                    if n == Q_SCALE and not first:
                        norm.scale_now(nc.gpsimd, c - 1)
                    if n == Q_FINISH and not last:
                        finish_step(c + 1, 1 - s)
                    if n == Q_LOW and not last:
                        low(c + 1, 1 - s)

            pool.sem_inc(hc_ready, HR)
            low(0, 0)
            finish_step(0, 0)
            over_chunks(pool, NCH, chunk)

        @block.vector
        def _(dve):
            def scaled_input(c, s, n):
                if n == 0:
                    dve.wait_ge(b_ready, c + 1)
                dve.wait_ge(rep_ready, c * NT + n + 1)
                dve.wait_ge(drive_ready, c * NT + n + 1)
                nc.vector.scalar_tensor_tensor(out=v[:, n % VB, :], in0=rep_ps[n % REP][:],
                                               scalar=inv_a[:, n:n + 1], in1=b_rep[:, s, :],
                                               op0=ALU.mult, op1=ALU.mult).then_inc(v_ready, 1)

            def driving(c, n):
                dve.wait_ge(v_ready, c * NT + n + 1 + REP)
                dve.wait_ge(decay_ready, c * NT + n + 1)
                dve.wait_ge(h_ready, c * NT + n + 1 + AB - BB)
                nc.vector.scalar_tensor_tensor(out=drive[:, n % BB, :], in0=decay[:, n % AB, :],
                                               scalar=-1.0, in1=v[:, n % VB, :],
                                               op0=ALU.add, op1=ALU.mult).then_inc(drive_ready, 1)

            def scan(c, n):
                dve.wait_ge(drive_ready, c * NT + n + 1 + VB)
                dve.wait_ge(hc_ready, c * NT + n + 1)
                if n % NQ == 0:
                    dve.wait_ge(carry_ready, c * (NT // NQ) + n // NQ + 1)
                nc.vector.tensor_tensor_scan(out=h[:, n % HR, :], data0=decay[:, n % AB, :],
                                             data1=drive[:, n % BB, :], initial=carry[:, n:n + 1],
                                             op0=ALU.mult, op1=ALU.add).then_inc(h_ready, 1)

            def keep_last_states(c, g):
                dve.wait_ge(h_ready, c * NT + g + NQ + AB)
                nc.vector.tensor_copy(carry[:, g:g + NQ], h[:, g % HR:g % HR + NQ, CH - 1]
                                      ).then_inc(carry_ready, 1)

            def residual(c):
                for half in range(2):
                    dve.wait_ge(y_ready, c * NT + TPB * (half + 1) + HC)
                    norm.add_residual(dve, c, half, y_ps[half][:])

            def chunk(c, s, first, last):
                for n in range(NT + 3):
                    if n < NT:
                        scaled_input(c, s, n)
                    if 0 <= n - 1 < NT:
                        driving(c, n - 1)
                    if 0 <= n - 2 < NT:
                        scan(c, n - 2)
                    if n >= 3 and (n - 3) % NQ == NQ - 1:
                        keep_last_states(c, n - 3 - (NQ - 1))
                    if not first:
                        if n == Q_RES:
                            residual(c - 1)
                        if n == Q_CENTRE:
                            norm.centre(dve, c - 1)

            dve.wait_ge(loaded, LOADS)
            nc.vector.reciprocal(inv_a[:], a_cols[:]).then_inc(const_ready, 1)
            nc.vector.tensor_tensor(step_bias[:], bias[:, 2:3], bias[:, 3:4], ALU.add).then_inc(const_ready, 1)
            nc.vector.memset(carry[:], 0.0).then_inc(const_ready, 1)
            nc.vector.tensor_copy(sel_rep[:], k["sel_rep"][:]).then_inc(const_ready, 1)
            dve.wait_ge(const_ready, 4)
            dve.sem_inc(v_ready, REP)
            dve.sem_inc(drive_ready, VB)
            dve.sem_inc(h_ready, AB)
            dve.sem_inc(carry_ready, NT // NQ)
            dve.sem_inc(norm.z_ready, norm.FREE)
            over_chunks(dve, NCH, chunk)
            residual(NCH - 1)
            norm.centre(dve, NCH - 1)
            norm.scale(dve, NCH - 1)


def layer0_experts(nc, xT, k, w, next_weights):
    T = xT.shape[2]
    NCH, NB = T // CH, T // P
    BPC = CH // P
    E1, _, PACK = w["experts"].shape
    D, NE, K = 2 * P, E1 - 1, 8
    F32R = mybir.dt.float32r
    WCOLS = 3 * D
    IN = 4
    LAG = 2
    WBUF = 3
    assert E1 % WBUF == 0 and E1 // WBUF >= 3
    with ExitStack() as ctx:
        def sb(name, shape, dt=F32):
            return ctx.enter_context(nc.sbuf_tensor("b_" + name, shape, dt))

        def sem(name):
            return ctx.enter_context(nc.semaphore("b_" + name))

        ps = [ctx.enter_context(nc.psum_tensor(f"b_ps{i}", [P, CH], F32)) for i in range(8)]
        pack = sb("pack", [P, WBUF, PACK])
        parts = [sb(f"pack_{n}", [P, WBUF, WCOLS], F32R) for n in ("high", "low")]
        gate_w = [[a[:, b, 0:D].rearrange("p (h i) -> p h i", h=2) for a in parts] for b in range(WBUF)]
        up_w = [[a[:, b, D:2 * D].rearrange("p (h i) -> p h i", h=2) for a in parts] for b in range(WBUF)]
        down_w = [[a[:, b, 2 * D:3 * D] for a in parts] for b in range(WBUF)]
        x_parts = [sb(f"x_{n}", [P, 2, T], F32R) for n in ("high", "low")]
        PARTS = ((0, 0), (0, 1), (1, 0))
        gate_b = [pack[:, b, 3 * D:3 * D + 1] for b in range(WBUF)]
        up_b = [pack[:, b, 3 * D + 1:3 * D + 2] for b in range(WBUF)]
        router_w = sb("router_w", [P, 2, NE])
        router_b = sb("router_b", [NE, 1])
        down_b = sb("down_b", [E1, D])
        aff = sb("aff", [P, 2, BPC, NE])
        top = sb("top", [P, 2, BPC, K])
        rest = sb("rest", [P, 2, BPC, NE])
        total = sb("total", [P, 2, BPC])
        w_c = sb("w_c", [P, 2, BPC, E1])
        w_all = sb("w_all", [P, NB, E1])
        acc = sb("acc", [P, NB, D])
        silu = sb("silu", [P, 2, CH])
        inner = sb("inner", [P, 2, CH])
        in_parts = [sb(f"inner_{n}", [P, IN, CH], F32R) for n in ("high", "low")]
        logit_t, w_t = silu[0:NE], inner[0:E1]

        loaded = sem("loaded")
        ones_ready = sem("ones_ready")
        logit_ready = sem("logit_ready")
        logit_kept = sem("logit_kept")
        logit_turned = sem("logit_turned")
        aff_ready = sem("aff_ready")
        top_ready = sem("top_ready")
        rest_ready = sem("rest_ready")
        total_ready = sem("total_ready")
        picked = sem("picked")
        w_ready = sem("w_ready")
        w_kept = sem("w_kept")
        w_turned = sem("w_turned")
        wt_ready = sem("wt_ready")
        bias_ready = sem("bias_ready")
        acc_started = sem("acc_started")
        pack_loaded = [sem(f"pack_loaded{b}") for b in range(WBUF)]
        x_high = sem("x_high")
        x_low = sem("x_low")
        w_high = sem("w_high")
        w_low = sem("w_low")
        in_high = sem("in_high")
        in_low = sem("in_low")
        gate_ready = sem("gate_ready")
        up_ready = sem("up_ready")
        silu_ready = sem("silu_ready")
        inner_ready = sem("inner_ready")
        down_ready = sem("down_ready")
        acc_ready = sem("acc_ready")
        turned = sem("turned")
        z_ready = sem("z_ready")
        mean_ready = sem("mean_ready")
        zc_ready = sem("zc_ready")
        sq_ready = sem("sq_ready")
        var_ready = sem("var_ready")
        log_var_ready = sem("log_var_ready")
        rstd_ready = sem("rstd_ready")
        x_ready = sem("x_ready")
        place = lambda c: acc[:, c * BPC:(c + 1) * BPC, :].rearrange("p b d -> p (b d)").rearrange(
            "p (h t) -> p h t", h=2)
        POOL_CHUNKS = [c for c in range(NCH) if c % 4 == 3]

        def scale(eng, ops, c):
            eng.wait_ge(rstd_ready, 1 + c // (NCH // 2))
            ops.tensor_tensor(xT[:, :, c * CH:(c + 1) * CH], xT[:, :, c * CH:(c + 1) * CH],
                              place(c)[:, 0:1].broadcast_to([P, 2, CH]), ALU.mult).then_inc(x_ready, 1)

        block = ctx.enter_context(nc.Block())
        LOADS = 3 * 16
        x_of = lambda half, c: xT[:, half, c * CH:(c + 1) * CH]

        def over_experts(eng, expert):
            for b in range(WBUF):
                expert(b, 0, b)
            with eng.Fori(1, E1 // WBUF - 1) as i:
                for b in range(WBUF):
                    expert(i * WBUF + b, i, b)
            for b in range(WBUF):
                expert(E1 - WBUF + b, E1 // WBUF - 1, b)

        def before(e, b, c, n):
            if c >= n:
                return e, b, c - n
            return None if isinstance(e, int) and e == 0 else (e - 1, (b - 1) % WBUF, c - n + NCH)

        @block.sync
        def _(sp):
            sp.dma_start(router_w[:], w["router_w"].rearrange("(h p) e -> p h e", p=P)).then_inc(loaded, 16)
            sp.dma_start(router_b[:], w["router_b"]).then_inc(loaded, 16)
            sp.dma_start(down_b[:], w["down_b"]).then_inc(loaded, 16)

            def expert(e, i, b):
                if not (isinstance(e, int) and e < WBUF):
                    sp.wait_ge(acc_ready, (e - WBUF + 1) * NCH * BPC + 2 * BPC)
                sp.dma_start(pack[:, b], w["experts"][bass.ds(e, 1)].rearrange("o p n -> p (o n)")
                             ).then_inc(pack_loaded[b], 16)

            over_experts(sp, expert)
            next_weights.load(sp)

        @block.tensor
        def _(pe):
            pe.wait_ge(loaded, LOADS)

            def logits(c):
                pe.wait_ge(logit_kept, c)
                for half in range(2):
                    last = nc.tensor.matmul(ps[0][0:NE, :], router_w[:, half, :], x_of(half, c),
                                            start=(half == 0), stop=(half == 1))
                last.then_inc(logit_ready, 1)

            def turn_logits(c):
                pe.wait_ge(logit_kept, c + 1)
                pe.wait_ge(aff_ready, c)
                for b in range(BPC):
                    last = nc.tensor.transpose(ps[1][:, b * NE:(b + 1) * NE],
                                               logit_t[:, c % 2, b * P:(b + 1) * P], k["ident"][0:NE, 0:NE])
                last.then_inc(logit_turned, 1)

            def start_sums(c):
                turn_bank, sum_banks = (ps[2], ps[3:5]) if c % 2 == 0 else (ps[5], ps[6:8])
                pe.wait_ge(w_ready, (c + 1) * BPC)
                if c >= 2:
                    pe.wait_ge(wt_ready, c - 1)
                    pe.wait_ge(acc_started, (c - 1) * 2)
                for b in range(BPC):
                    last = nc.tensor.transpose(turn_bank[0:E1, b * P:(b + 1) * P], w_c[:, c % 2, b, :], k["ident"])
                last.then_inc(w_turned, 1)
                pe.wait_ge(wt_ready, c + 1)
                for b in range(BPC):
                    last = nc.tensor.matmul(sum_banks[b // 2][:, b % 2 * D:b % 2 * D + D],
                                            w_t[:, c % 2, b * P:(b + 1) * P], down_b[:], start=True, stop=True)
                last.then_inc(bias_ready, 1)

            for c in range(NCH + 3):
                if c < NCH:
                    logits(c)
                if 1 <= c <= NCH:
                    turn_logits(c - 1)
                if c >= 3:
                    start_sums(c - 3)
            pe.wait_ge(acc_started, NCH * 2)

            def gate_up(e, b, c):
                q = e * NCH + c
                if c == 0:
                    pe.wait_ge(w_high, e + 1)
                    pe.wait_ge(w_low, e + 1)
                if isinstance(e, int) and e == 0:
                    pe.wait_ge(x_high, c + 1)
                    pe.wait_ge(x_low, c + 1)
                for weights, bank, left, done in ((gate_w, ps[c % 2], silu_ready, gate_ready),
                                                  (up_w, ps[2 + c % 2], inner_ready, up_ready)):
                    pe.wait_ge(left, q + 1)
                    for n, (half, (i, j)) in enumerate((half, p) for half in range(2) for p in PARTS):
                        last = nc.tensor.matmul(bank[:], weights[b][i][:, half, :],
                                                x_parts[j][:, half, c * CH:(c + 1) * CH],
                                                start=(n == 0), stop=(n == 5))
                    last.then_inc(done, 1)

            def down(e, b, c):
                q = e * NCH + c
                pe.wait_ge(in_high, q + 1)
                pe.wait_ge(in_low, q + 1)
                pe.wait_ge(acc_ready, (q + 1) * BPC)
                for t in range(BPC):
                    for n, (i, j) in enumerate(PARTS):
                        last = nc.tensor.matmul(ps[4 + 2 * (c % 2) + t // 2][:, t % 2 * D:t % 2 * D + D],
                                                in_parts[i][:, c % IN, t * P:(t + 1) * P], down_w[b][j],
                                                start=(n == 0), stop=(n == 2))
                last.then_inc(down_ready, 1)

            def expert(e, i, b):
                for c in range(NCH):
                    gate_up(e, b, c)
                    if at := before(e, b, c, LAG):
                        down(*at)

            pe.sem_inc(down_ready, IN)
            over_experts(pe, expert)
            for n in range(LAG):
                down(E1 - 1, (E1 - 1) % WBUF, NCH - LAG + n)

            def turn(c):
                if c >= 2:
                    pe.wait_ge(z_ready, (c - 1) * 2)
                for half in range(2):
                    for b in range(BPC):
                        last = nc.tensor.transpose(ps[c % 2 * 2 + half][:, b * P:(b + 1) * P],
                                                   acc[:, c * BPC + b, half * P:(half + 1) * P], k["ident"])
                    last.then_inc(turned, 1)

            def average(c, bank, done):
                for half in range(2):
                    last = nc.tensor.matmul(bank[:], k["avg"], place(c)[:, half], start=(half == 0), stop=(half == 1))
                last.then_inc(done, 1)

            pe.wait_ge(acc_ready, E1 * NCH * BPC + 2 * BPC)
            for c in range(NCH + 2):
                if c < NCH:
                    turn(c)
                if 1 <= c <= NCH:
                    if c >= 3:
                        pe.wait_ge(zc_ready, (c - 2) * 2)
                    pe.wait_ge(z_ready, c * 2)
                    average(c - 1, ps[4 + (c - 1) % 2], mean_ready)
                if c >= 2:
                    if c >= 4:
                        pe.wait_ge(log_var_ready, c - 3)
                    pe.wait_ge(sq_ready, c - 1)
                    average(c - 2, ps[6 + c % 2], var_ready)

        @block.scalar
        def _(act):
            act.wait_ge(loaded, LOADS)

            def keep_logits(c):
                act.wait_ge(logit_ready, c + 1)
                if c >= 2:
                    act.wait_ge(logit_turned, c - 1)
                nc.scalar.activation(logit_t[:, c % 2, :], ps[0][0:NE, :], ACT.Identity,
                                     bias=router_b[:]).then_inc(logit_kept, 1)

            def affinity(c):
                act.wait_ge(logit_turned, c + 1)
                if c >= 2:
                    act.wait_ge(picked, c - 1)
                nc.scalar.activation(aff[:, c % 2], ps[1][:, 0:BPC * NE].rearrange("p (b e) -> p b e", b=BPC),
                                     ACT.Sigmoid).then_inc(aff_ready, 1)

            def keep_weights(c):
                act.wait_ge(w_turned, c + 1)
                if c >= 2:
                    act.wait_ge(bias_ready, c - 1)
                nc.scalar.copy(w_t[:, c % 2, :], ps[2 if c % 2 == 0 else 5][0:E1, :]).then_inc(wt_ready, 1)

            def start_acc(c):
                act.wait_ge(bias_ready, c + 1)
                for i in range(BPC // 2):
                    b, bank = c * BPC + 2 * i, ps[(3 if c % 2 == 0 else 6) + i]
                    nc.scalar.copy(acc[:, b:b + 2, :], bank[:].rearrange("p (b d) -> p b d", b=2)
                                   ).then_inc(acc_started, 1)

            for c in range(NCH + 4):
                if c < NCH:
                    keep_logits(c)
                if 1 <= c <= NCH:
                    affinity(c - 1)
                if 3 <= c < NCH + 3:
                    keep_weights(c - 3)
                if c < NCH:
                    nc.scalar.copy(x_parts[0][:, :, c * CH:(c + 1) * CH], xT[:, :, c * CH:(c + 1) * CH]
                                   ).then_inc(x_high, 1)
                if c >= 4:
                    start_acc(c - 4)

            def split_weights(e, i, b):
                act.wait_ge(pack_loaded[b], i * 16 + 16)
                if not (isinstance(e, int) and e < WBUF):
                    act.wait_ge(down_ready, (e - WBUF + 1) * NCH + IN)
                nc.scalar.copy(parts[0][:, b, :], pack[:, b, 0:WCOLS]).then_inc(w_high, 1)

            def split_inner(e, b, c):
                q = e * NCH + c
                act.wait_ge(inner_ready, q + 1 + 2)
                act.wait_ge(down_ready, q + 1)
                nc.scalar.copy(in_parts[0][:, c % IN, :], inner[:, c % 2, :]).then_inc(in_high, 1)

            def expert(e, i, b):
                for c in range(NCH):
                    q = e * NCH + c
                    act.wait_ge(gate_ready, q + 1)
                    act.wait_ge(inner_ready, q + 1)
                    nc.scalar.activation(silu[:, c % 2, :], ps[c % 2][:], ACT.Silu,
                                         bias=gate_b[b]).then_inc(silu_ready, 1)
                    if at := before(e, b, c, 1):
                        split_inner(*at)
                    if c == NCH // 2 and not (isinstance(e, int) and e == E1 - 1):
                        if b + 1 < WBUF:
                            split_weights(e + 1, i, b + 1)
                        else:
                            split_weights(e + 1, i + 1, 0)

            split_weights(0, 0, 0)
            act.sem_inc(silu_ready, 2)
            over_experts(act, expert)
            split_inner(E1 - 1, (E1 - 1) % WBUF, NCH - 1)
            for c in range(NCH + 1):
                if c < NCH:
                    act.wait_ge(zc_ready, (c + 1) * 2)
                    nc.scalar.activation(place(c), xT[:, :, c * CH:(c + 1) * CH], ACT.Square).then_inc(sq_ready, 1)
                if c >= 1:
                    act.wait_ge(var_ready, c)
                    nc.scalar.activation(place(c - 1)[:, 0], ps[6 + (c - 1) % 2][:], ACT.Ln, bias=k["eps"]
                                         ).then_inc(log_var_ready, 1)
            act.wait_ge(log_var_ready, NCH)
            for half in range(2):
                rows = acc[:, half * NB // 2:(half + 1) * NB // 2, :].rearrange(
                    "p (c b) d -> p c (b d)", b=BPC)[:, :, 0:CH]
                nc.scalar.activation(rows, rows, ACT.Exp, scale=-0.5).then_inc(rstd_ready, 1)

        @block.gpsimd
        def _(pool):
            for c in range(NCH):
                pool.wait_ge(x_high, c + 1)
                cols = slice(c * CH, (c + 1) * CH)
                nc.gpsimd.tensor_tensor(x_parts[1][:, :, cols], xT[:, :, cols],
                                        x_parts[0][:, :, cols].bitcast(F32), ALU.subtract).then_inc(x_low, 1)

            def split_weights(e, b):
                pool.wait_ge(w_high, e + 1)
                nc.gpsimd.tensor_tensor(parts[1][:, b, :], pack[:, b, 0:WCOLS], parts[0][:, b, :].bitcast(F32),
                                        ALU.subtract).then_inc(w_low, 1)

            def expert(e, i, b):
                for c in range(NCH):
                    pool.wait_ge(in_high, e * NCH + c + 1)
                    nc.gpsimd.tensor_tensor(in_parts[1][:, c % IN, :], inner[:, c % 2, :],
                                            in_parts[0][:, c % IN, :].bitcast(F32), ALU.subtract
                                            ).then_inc(in_low, 1)
                    if c == NCH // 2 and not (isinstance(e, int) and e == E1 - 1):
                        split_weights(e + 1, (b + 1) % WBUF)

            split_weights(0, 0)
            over_experts(pool, expert)
            for c in POOL_CHUNKS:
                scale(pool, nc.gpsimd, c)

        @block.vector
        def _(dve):
            nc.vector.memset(w_c[:, :, :, NE:E1], 1.0).then_inc(ones_ready, 1)
            dve.wait_ge(ones_ready, 1)
            dve.sem_inc(inner_ready, 2)
            dve.sem_inc(acc_ready, 2 * BPC)

            def weigh(c):
                s = c % 2
                dve.wait_ge(aff_ready, c + 1)
                for b in range(BPC):
                    nc.vector.max(top[:, s, b, :], aff[:, s, b, :]).then_inc(top_ready, 1)
                dve.wait_ge(top_ready, (c + 1) * BPC)
                for b in range(BPC):
                    nc.vector.match_replace(out=rest[:, s, b, :], in_to_replace=top[:, s, b, :],
                                            in_values=aff[:, s, b, :], imm_value=0.0).then_inc(rest_ready, 1)
                nc.vector.reduce_sum(total[:, s, :], top[:, s], axis=AX_X).then_inc(total_ready, 1)
                dve.wait_ge(total_ready, c * 3 + 1)
                nc.vector.tensor_scalar(total[:, s, :], total[:, s, :], 1e-9, None, ALU.add).then_inc(total_ready, 1)
                dve.wait_ge(total_ready, c * 3 + 2)
                nc.vector.reciprocal(total[:, s, :], total[:, s, :]).then_inc(total_ready, 1)
                dve.wait_ge(rest_ready, (c + 1) * BPC)
                nc.vector.tensor_tensor(rest[:, s], aff[:, s], rest[:, s], ALU.subtract).then_inc(picked, 1)
                dve.wait_ge(total_ready, c * 3 + 3)
                dve.wait_ge(picked, c + 1)
                if c >= 2:
                    dve.wait_ge(w_turned, c - 1)
                    dve.wait_ge(w_kept, c - 1)
                for b in range(BPC):
                    nc.vector.tensor_scalar(w_c[:, s, b, 0:NE], rest[:, s, b, :], total[:, s, b:b + 1], None,
                                            ALU.mult).then_inc(w_ready, 1)
                dve.wait_ge(w_ready, (c + 1) * BPC)
                nc.vector.tensor_copy(w_all[:, c * BPC:(c + 1) * BPC, :], w_c[:, s]).then_inc(w_kept, 1)

            for c in range(NCH):
                weigh(c)
            dve.wait_ge(w_kept, NCH)
            dve.wait_ge(acc_started, 2 * NCH)

            def gate_times_up(e, b, c):
                q = e * NCH + c
                dve.wait_ge(up_ready, q + 1)
                dve.wait_ge(silu_ready, q + 1 + 2)
                if not (isinstance(e, int) and e == 0 and c < 2):
                    dve.wait_ge(in_low, q - 1)
                nc.vector.scalar_tensor_tensor(out=inner[:, c % 2, :], in0=ps[2 + c % 2][:], scalar=up_b[b],
                                               in1=silu[:, c % 2, :], op0=ALU.add, op1=ALU.mult
                                               ).then_inc(inner_ready, 1)

            def accumulate(e, b, c):
                q = e * NCH + c
                dve.wait_ge(down_ready, q + 1 + IN)
                if not (isinstance(e, int) and e == 0):
                    dve.wait_ge(acc_ready, (q - NCH + 1) * BPC + 2 * BPC)
                for t in range(BPC):
                    tb = c * BPC + t
                    nc.vector.scalar_tensor_tensor(
                        out=acc[:, tb, :], in0=ps[4 + 2 * (c % 2) + t // 2][:, t % 2 * D:t % 2 * D + D],
                        scalar=w_all[:, tb, bass.ds(e, 1)], in1=acc[:, tb, :], op0=ALU.mult, op1=ALU.add
                    ).then_inc(acc_ready, 1)

            def expert(e, i, b):
                for c in range(NCH):
                    gate_times_up(e, b, c)
                    if at := before(e, b, c, LAG):
                        accumulate(*at)

            over_experts(dve, expert)
            for n in range(LAG):
                accumulate(E1 - 1, (E1 - 1) % WBUF, NCH - LAG + n)

            for c in range(NCH + 1):
                if c < NCH:
                    for half in range(2):
                        dve.wait_ge(turned, c * 2 + 2)
                        nc.vector.tensor_tensor(place(c)[:, half], x_of(half, c), ps[c % 2 * 2 + half][:],
                                                ALU.add).then_inc(z_ready, 1)
                if c >= 1:
                    dve.wait_ge(mean_ready, c)
                    for half in range(2):
                        nc.vector.tensor_tensor(x_of(half, c - 1), place(c - 1)[:, half], ps[4 + (c - 1) % 2][:],
                                                ALU.subtract).then_inc(zc_ready, 1)
            for c in range(NCH):
                if c not in POOL_CHUNKS:
                    scale(dve, nc.vector, c)


class ScanWeights:

    LOADS = 7 * 16

    def __init__(self, nc, ctx, w):
        D, DI = 2 * P, w["out_w"].shape[0]
        NM, RANK = DI // P, w["dt_w"].shape[0]

        def sb(name, shape):
            return ctx.enter_context(nc.sbuf_tensor("c_" + name, shape, F32))

        in_w = sb("in_w", [P, 2, 2 * DI])
        x_w = sb("x_w", [P, NM, RANK + 2 * N_STATE])
        dt_w = sb("dt_w", [RANK, DI])
        out_w = sb("out_w", [P, NM, D])
        conv_w = sb("conv_w", [P, NM, w["conv_w"].shape[2]])
        vecs = sb("vecs", [P, 3, NM])
        a_cols = sb("a_cols", [P, N_STATE * NM])
        self.w, self.loaded = w, ctx.enter_context(nc.semaphore("c_loaded"))
        self.all = in_w, x_w, dt_w, out_w, conv_w, vecs, a_cols, self.loaded

    def load(self, sp):
        w = self.w
        in_w, x_w, dt_w, out_w, conv_w, vecs, a_cols, loaded = self.all
        sp.dma_start(in_w[:], w["in_w"].rearrange("(h p) n -> p h n", p=P)).then_inc(loaded, 16)
        sp.dma_start(x_w[:], w["x_w"].rearrange("(m p) n -> p m n", p=P)).then_inc(loaded, 16)
        sp.dma_start(dt_w[:], w["dt_w"]).then_inc(loaded, 16)
        sp.dma_start(out_w[:], w["out_w"].rearrange("(m p) n -> p m n", p=P)).then_inc(loaded, 16)
        sp.dma_start(conv_w[:], w["conv_w"]).then_inc(loaded, 16)
        sp.dma_start(vecs[:], w["vecs"]).then_inc(loaded, 16)
        sp.dma_start(a_cols[:], w["a_log_cols"]).then_inc(loaded, 16)


def layer1_scan(nc, xT, k, w, weights):
    T = xT.shape[2]
    NCH = T // CH
    D, DI = 2 * P, w["out_w"].shape[0]
    NM = DI // P
    RANK = w["dt_w"].shape[0]
    TAPS = w["conv_w"].shape[2]
    HALO = TAPS - 1
    PAIR = 2
    NU = N_STATE * NM // PAIR
    NT = NU * PAIR
    DEC, VB, HR, HC, BC = 8, 2, 4, 4, 4
    GATE, X_DBL, DT, ITEMS = NM, 2 * NM, 2 * NM + 1, 3 * NM + 1
    UPN = NM // PAIR
    Q_SKIP, Q_GATE, Q_OUT, Q_RES, Q_MEAN, Q_CENTRE, Q_SQUARE, Q_VAR, Q_SCALE = 3, 2, 3, 10, 11, 15, 17, 13, 32
    Q_SILU, Q_EXP, Q_LOG, Q_HALO, Q_ERR, Q_DT, Q_DTU = 19, 25, 31, 15, 27, 29, 26
    X_PE, G_PE, D_PE, X_ACT, G_ACT, D_ACT = 4, 8, 14, 9, 15, 21
    AT_PE, AT_ACT = ({**{x + i: (i,) for i in range(NM)}, **{g + i: (GATE + i,) for i in range(NM)},
                      **{d + i: (X_DBL + i,) for i in range(1 + NM)}}
                     for x, g, d in ((X_PE, G_PE, D_PE), (X_ACT, G_ACT, D_ACT)))
    AT_TAP = {8: ((0, 1),), 9: ((0, 2), (1, 1)), 10: ((0, 3), (1, 2)), 11: ((1, 3), (2, 1)), 12: ((2, 2), (3, 1)),
              13: ((2, 3), (3, 2)), 14: ((3, 3),)}
    with ExitStack() as ctx:
        def sb(name, shape):
            return ctx.enter_context(nc.sbuf_tensor("c_" + name, shape, F32))

        def sem(name):
            return ctx.enter_context(nc.semaphore("c_" + name))

        ps = [ctx.enter_context(nc.psum_tensor(f"c_ps{i}", [P, CH], F32)) for i in range(8)]
        y_ps, work_ps, out_ps, norm_ps = ps[0:4], ps[4:6], ps[6:8], ps[7]
        bc_dram = nc.dram_tensor("c_bc_scratch", (2, 2, N_STATE, CH), F32, kind="Internal").ap()
        in_w, x_w, dt_w, out_w, conv_w, vecs, a_cols, loaded = weights.all
        conv_b, dt_b, d_skip = vecs[:, 0], vecs[:, 1], vecs[:, 2]
        xin = sb("xin", [P, NM, HALO + CH])
        u = sb("u", [P, 2, NM, CH])
        gate = sb("gate", [P, NM, CH])
        dt = sb("dt", [P, 2, NM, CH])
        dtu = sb("dtu", [P, 2, NM, CH])
        e = sb("e", [P, NM, CH])
        x_dbl = sb("x_dbl", [RANK + 2 * N_STATE, CH])
        b_rep = sb("b_rep", [P, BC, CH])
        c_rep = sb("c_rep", [P, BC, CH])
        decay = sb("decay", [P, DEC, CH])
        v = sb("v", [P, VB, PAIR, CH])
        h = sb("h", [P, HR, PAIR, CH])
        hc = sb("hc", [P, HC, PAIR, CH])
        carry = sb("carry", [P, NT])

        a_ready = sem("a_ready")
        work_ready = sem("work_ready")
        work_left = sem("work_left")
        relu_ready = sem("relu_ready")
        tap0_ready = sem("tap0_ready")
        taps_ready = sem("taps_ready")
        halo_ready = sem("halo_ready")
        u_ready = sem("u_ready")
        gate_ready = sem("gate_ready")
        e_ready = sem("e_ready")
        w_ready = sem("w_ready")
        err_ready = sem("err_ready")
        ln_ready = sem("ln_ready")
        log_ready = sem("log_ready")
        dt_ready = sem("dt_ready")
        dtu_ready = sem("dtu_ready")
        bc_stored = sem("bc_stored")
        b_loaded = [sem(f"b_loaded{i}") for i in range(BC)]
        c_loaded = [sem(f"c_loaded{i}") for i in range(BC)]
        decay_ready = sem("decay_ready")
        v_ready = sem("v_ready")
        h_ready = sem("h_ready")
        carry_ready = sem("carry_ready")
        hc_ready = sem("hc_ready")
        y_ready = sem("y_ready")
        skip_ready = sem("skip_ready")
        gated = sem("gated")
        out_ready = sem("out_ready")
        norm = Norm(nc, sb, sem, norm_ps[:], k, xT)

        block = ctx.enter_context(nc.Block())
        LOADS = ScanWeights.LOADS

        @block.sync
        def _(sp):
            def store_bc(c, s):
                sp.wait_ge(work_left, c * ITEMS + X_DBL + 1)
                sp.dma_start(bc_dram[s].rearrange("o n t -> (o n) t"), x_dbl[RANK:RANK + 2 * N_STATE, :]
                             ).then_inc(bc_stored, 16)

            def spread(c, s, n):
                if n == 0:
                    sp.wait_ge(bc_stored, c * 16 + 16)
                if not (isinstance(c, int) and c == 0 and n < BC):
                    sp.wait_ge(v_ready, c * NU + (n - BC + 1) * UPN)
                sp.dma_start(b_rep[:, n % BC], bc_dram[s, 0, n:n + 1, :].broadcast_to([P, CH])
                             ).then_inc(b_loaded[n % BC], 16)
                if not (isinstance(c, int) and c == 0 and n < BC):
                    sp.wait_ge(hc_ready, c * NU + (n - BC + 1) * UPN + HR)
                sp.dma_start(c_rep[:, n % BC], bc_dram[s, 1, n:n + 1, :].broadcast_to([P, CH])
                             ).then_inc(c_loaded[n % BC], 16)

            def chunk(c, s, first, last):
                for n in range(N_STATE):
                    spread(c, s, n)
                    if n == N_STATE - BC and not last:
                        store_bc(c + 1, 1 - s)

            store_bc(0, 0)
            over_chunks(sp, NCH, chunk)

        @block.tensor
        def _(pe):
            def product(r, i, s, last=False):
                if not (isinstance(r, int) and r == 0 and i < 2):
                    pe.wait_ge(work_left, r * ITEMS + i - 1)
                    if i < 2 or last and i < GATE + 2:
                        pe.wait_ge(relu_ready, r * NM)
                out = work_ps[(i + s) % 2]
                if i < X_DBL:
                    at = r if i < GATE else r - 1
                    for half in range(2):
                        done = nc.tensor.matmul(out[:], in_w[:, half, i * P:(i + 1) * P],
                                                xT[:, half, bass.ts(at, CH)],
                                                start=(half == 0), stop=(half == 1))
                elif i == X_DBL:
                    pe.wait_ge(u_ready, r + 1)
                    for m in range(NM):
                        done = nc.tensor.matmul(out[0:RANK + 2 * N_STATE, :], x_w[:, m, :], u[:, s, m, :],
                                                start=(m == 0), stop=(m == NM - 1))
                else:
                    m = i - DT
                    if m == 0:
                        pe.wait_ge(work_left, r * ITEMS + X_DBL + 1)
                    if m >= 2:
                        pe.wait_ge(relu_ready, r * NM + m - 1)
                    done = nc.tensor.matmul(out[:], dt_w[:, m * P:(m + 1) * P], x_dbl[0:RANK, :],
                                            start=True, stop=True)
                done.then_inc(work_ready, 1)

            def add_states(c, q):
                n, pair = q // UPN, q % UPN
                if n == 0:
                    pe.wait_ge(skip_ready, c * NM + (pair + 1) * PAIR)
                pe.wait_ge(hc_ready, c * NU + q + 1 + HR)
                for m in range(PAIR):
                    last = nc.tensor.matmul(y_ps[pair * PAIR + m][:], k["ident"], hc[:, q % HC, m, :],
                                            start=(n == 0), stop=(n == N_STATE - 1))
                last.then_inc(y_ready, 1)

            def project_out(c, m):
                if m == 0:
                    pe.wait_ge(norm.z_ready, c * 2 + norm.FREE)
                    pe.wait_ge(norm.log_ready, c)
                pe.wait_ge(gated, c * NM + m + 1)
                for half in range(2):
                    done = nc.tensor.matmul(out_ps[half][:], out_w[:, m, half * P:(half + 1) * P],
                                            gate[:, m, :], start=(m == 0), stop=(m == NM - 1))
                if m == NM - 1:
                    done.then_inc(out_ready, 1)

            def chunk(c, s, first, last):
                for q in range(NU):
                    if q >= 1:
                        add_states(c, q - 1)
                    elif not first:
                        add_states(c - 1, NU - 1)
                    if not first:
                        if Q_OUT <= q < Q_OUT + NM:
                            project_out(c - 1, q - Q_OUT)
                        if q == Q_MEAN:
                            norm.mean(pe, c - 1)
                        if q == Q_VAR:
                            norm.variance(pe, c - 1)
                    for i in AT_PE.get(q, ()):
                        if GATE <= i < X_DBL or not last:
                            product(c + 1, i, 1 - s, last)
                        elif i == 0:
                            pe.wait_ge(work_ready, (c + 1) * ITEMS)
                            pe.sem_inc(work_ready, GATE)

            pe.wait_ge(loaded, LOADS)
            pe.sem_inc(y_ready, HC)
            for i in range(GATE):
                product(0, i, 0)
            pe.wait_ge(work_ready, GATE)
            pe.sem_inc(work_ready, X_DBL - GATE)
            for i in range(X_DBL, ITEMS):
                product(0, i, 0)
            over_chunks(pe, NCH, chunk)
            add_states(NCH - 1, NU - 1)
            for m in range(NM):
                project_out(NCH - 1, m)
            norm.mean(pe, NCH - 1)
            norm.variance(pe, NCH - 1)

        @block.scalar
        def _(act):
            def leave(r, i, s):
                act.wait_ge(work_ready, r * ITEMS + i + 1)
                src = work_ps[(i + s) % 2]
                if i < GATE:
                    if i == 0:
                        act.wait_ge(halo_ready, r + 1)
                        if not (isinstance(r, int) and r < 2):
                            act.wait_ge(gated, (r - 1) * NM)
                    nc.scalar.copy(xin[:, i, HALO:], src[:]).then_inc(work_left, 1)
                    act.wait_ge(work_left, r * ITEMS + i + 1)
                    nc.scalar.activation(u[:, s, i, :], xin[:, i, 0:CH], ACT.Identity,
                                         scale=conv_w[:, i, 0:1], bias=conv_b[:, i:i + 1]
                                         ).then_inc(tap0_ready, 1)
                elif i < X_DBL:
                    if i == GATE and not (isinstance(r, int) and r < 2):
                        act.wait_ge(out_ready, r - 1)
                    nc.scalar.copy(gate[:, i - GATE, :], src[:]).then_inc(work_left, 1)
                elif i == X_DBL:
                    act.wait_ge(bc_stored, r * 16)
                    nc.scalar.copy(x_dbl[:], src[0:RANK + 2 * N_STATE, :]).then_inc(work_left, 1)
                else:
                    m = i - DT
                    if m == 0:
                        act.wait_ge(log_ready, r)
                        act.wait_ge(dt_ready, r)
                    nc.scalar.activation(dt[:, s, m, :], src[:], ACT.Relu, bias=dt_b[:, m:m + 1]
                                         ).then_inc(relu_ready, 1)
                    nc.scalar.activation(e[:, m, :], src[:], ACT.Abs, bias=dt_b[:, m:m + 1]
                                         ).then_inc(work_left, 1)

            def activate_u(r, s):
                act.wait_ge(taps_ready, (r + 1) * HALO * NM)
                nc.scalar.activation(u[:, s], u[:, s], ACT.Silu).then_inc(u_ready, 1)

            def activate_gate(c):
                act.wait_ge(work_left, (c + 1) * ITEMS + X_DBL)
                nc.scalar.activation(gate[:], gate[:], ACT.Silu).then_inc(gate_ready, 1)

            def exp_abs(c, s):
                act.wait_ge(work_left, (c + 1) * ITEMS)
                nc.scalar.activation(e[:], e[:], ACT.Exp, scale=-1.0).then_inc(e_ready, 1)
                act.wait_ge(e_ready, c + 1)
                nc.scalar.activation(dtu[:, s], e[:], ACT.Identity, bias=1.0).then_inc(w_ready, 1)

            def log(c, s):
                act.wait_ge(err_ready, c + 1)
                nc.scalar.activation(e[:], e[:], ACT.Ln, bias=1.0).then_inc(ln_ready, 1)

            def chunk(c, s, first, last):
                act.wait_ge(dt_ready, c + 1)
                for q in range(NU):
                    for m in range(PAIR):
                        i = q * PAIR + m
                        act.wait_ge(h_ready, c * NT + i + 1)
                        nc.scalar.activation(decay[:, i % DEC, :], dt[:, s, q % UPN * PAIR + m, :], ACT.Exp,
                                             scale=a_cols[:, i:i + 1]).then_inc(decay_ready, 1)
                    for i in AT_ACT.get(q, ()):
                        if GATE <= i < X_DBL or not last:
                            leave(c + 1, i, 1 - s)
                        elif i == 0:
                            act.wait_ge(work_left, (c + 1) * ITEMS)
                            act.sem_inc(work_left, GATE)
                    if q == Q_SILU:
                        if not last:
                            activate_u(c + 1, 1 - s)
                        activate_gate(c)
                    if q == Q_EXP and not last:
                        exp_abs(c + 1, 1 - s)
                    if q == Q_LOG and not last:
                        log(c + 1, 1 - s)
                    if q == Q_LOG and not first:
                        norm.deviation(act, c - 1)
                    if not first:
                        if q == Q_SQUARE:
                            norm.square(act, c - 1)

            act.wait_ge(loaded, LOADS)
            nc.scalar.activation(a_cols[:], a_cols[:], ACT.Exp).then_inc(a_ready, 1)
            act.wait_ge(a_ready, 4)
            for i in range(GATE):
                leave(0, i, 0)
            act.wait_ge(work_left, GATE)
            act.sem_inc(work_left, X_DBL - GATE)
            activate_u(0, 0)
            for i in range(X_DBL, ITEMS):
                leave(0, i, 0)
            exp_abs(0, 0)
            log(0, 0)
            over_chunks(act, NCH, chunk)
            norm.square(act, NCH - 1)
            norm.deviation(act, NCH - 1)

        @block.gpsimd
        def _(pool):
            def weigh_input(c, s, m):
                pool.wait_ge(dt_ready, c + 1)
                pool.wait_ge(u_ready, c + 1)
                nc.gpsimd.tensor_tensor(dtu[:, s, m], dt[:, s, m], u[:, s, m], ALU.mult).then_inc(dtu_ready, 1)

            def apply_gate(c, s, m):
                pool.wait_ge(skip_ready, c * NM + NM + m + 1)
                pool.wait_ge(gate_ready, c + 1)
                nc.gpsimd.tensor_tensor(gate[:, m], gate[:, m], u[:, s, m], ALU.mult).then_inc(gated, 1)

            def chunk(c, s, first, last):
                for q in range(NU):
                    n = q // UPN
                    if q % UPN == 0:
                        pool.wait_ge(c_loaded[n % BC], (c * (N_STATE // BC) + n // BC + 1) * 16)
                    pool.wait_ge(h_ready, c * NT + (q + 1) * PAIR + DEC)
                    pool.wait_ge(y_ready, c * NU + q + 1)
                    nc.gpsimd.tensor_tensor(hc[:, q % HC], h[:, q % HR],
                                            c_rep[:, n % BC].unsqueeze(1).broadcast_to([P, PAIR, CH]),
                                            ALU.mult).then_inc(hc_ready, 1)
                    if Q_GATE <= q < Q_GATE + NM and not first:
                        apply_gate(c - 1, 1 - s, q - Q_GATE)
                    if Q_DTU <= q < Q_DTU + NM and not last:
                        weigh_input(c + 1, 1 - s, q - Q_DTU)

            pool.sem_inc(hc_ready, HR)
            for m in range(NM):
                weigh_input(0, 0, m)
            over_chunks(pool, NCH, chunk)
            for m in range(NM):
                apply_gate(NCH - 1, 1, m)

        @block.vector
        def _(dve):
            def tap(c, s, m, j):
                if j == 1:
                    dve.wait_ge(tap0_ready, c * NM + m + 1)
                else:
                    dve.wait_ge(taps_ready, c * HALO * NM + m * HALO + j - 1)
                nc.vector.scalar_tensor_tensor(out=u[:, s, m, :], in0=xin[:, m, j:j + CH],
                                               scalar=conv_w[:, m, j:j + 1], in1=u[:, s, m, :],
                                               op0=ALU.mult, op1=ALU.add).then_inc(taps_ready, 1)

            def keep_halo(c):
                dve.wait_ge(taps_ready, (c + 1) * HALO * NM)
                dve.wait_ge(tap0_ready, (c + 1) * NM)
                nc.vector.tensor_copy(xin[:, :, 0:HALO], xin[:, :, CH:CH + HALO]).then_inc(halo_ready, 1)

            def log_error(c, s):
                dve.wait_ge(w_ready, c + 1)
                nc.vector.scalar_tensor_tensor(out=dtu[:, s], in0=dtu[:, s], scalar=-1.0, in1=e[:],
                                               op0=ALU.add, op1=ALU.subtract).then_inc(err_ready, 1)

            def finish_dt(c, s):
                dve.wait_ge(err_ready, c + 1)
                dve.wait_ge(ln_ready, c + 1)
                nc.vector.tensor_tensor(e[:], e[:], dtu[:, s], ALU.subtract).then_inc(log_ready, 1)
                dve.wait_ge(log_ready, c + 1)
                dve.wait_ge(relu_ready, (c + 1) * NM)
                nc.vector.tensor_tensor(dt[:, s], dt[:, s], e[:], ALU.add).then_inc(dt_ready, 1)

            def spread_input(c, s, q):
                n, pair = q // UPN, q % UPN
                if n == 0:
                    dve.wait_ge(dtu_ready, c * NM + (pair + 1) * PAIR)
                if pair == 0:
                    dve.wait_ge(b_loaded[n % BC], (c * (N_STATE // BC) + n // BC + 1) * 16)
                dve.wait_ge(h_ready, c * NT + q * PAIR + DEC - PAIR)
                nc.vector.tensor_tensor(v[:, q % VB], dtu[:, s, pair * PAIR:(pair + 1) * PAIR, :],
                                        b_rep[:, n % BC].unsqueeze(1).broadcast_to([P, PAIR, CH]),
                                        ALU.mult).then_inc(v_ready, 1)

            def scan(c, q):
                dve.wait_ge(v_ready, c * NU + q + 1)
                dve.wait_ge(hc_ready, c * NU + q + 1)
                dve.wait_ge(carry_ready, c * NU + q - HR + 1 + NU)
                for m in range(PAIR):
                    i = q * PAIR + m
                    dve.wait_ge(decay_ready, c * NT + i + 1)
                    nc.vector.tensor_tensor_scan(out=h[:, q % HR, m, :], data0=decay[:, i % DEC, :],
                                                 data1=v[:, q % VB, m, :], initial=carry[:, i:i + 1],
                                                 op0=ALU.mult, op1=ALU.add).then_inc(h_ready, 1)

            def keep_last_states(c, q):
                dve.wait_ge(h_ready, c * NT + (q + 1) * PAIR + DEC)
                nc.vector.tensor_copy(carry[:, q * PAIR:(q + 1) * PAIR], h[:, q % HR, :, CH - 1]
                                      ).then_inc(carry_ready, 1)

            def skip(c, s):
                dve.wait_ge(y_ready, (c + 1) * NU + HC)
                for m in range(NM):
                    nc.vector.scalar_tensor_tensor(out=u[:, s, m, :], in0=u[:, s, m, :],
                                                   scalar=d_skip[:, m:m + 1], in1=y_ps[m][:],
                                                   op0=ALU.mult, op1=ALU.add).then_inc(skip_ready, 1)

            def residual(c):
                dve.wait_ge(out_ready, c + 1)
                for half in range(2):
                    norm.add_residual(dve, c, half, out_ps[half][:])

            def chunk(c, s, first, last):
                for q in range(NU + 2):
                    if q < NU:
                        spread_input(c, s, q)
                    if 1 <= q <= NU:
                        scan(c, q - 1)
                    if q >= 2:
                        keep_last_states(c, q - 2)
                    if not first:
                        if q == Q_SKIP:
                            skip(c - 1, 1 - s)
                        if q == Q_RES:
                            residual(c - 1)
                        if q == Q_CENTRE:
                            norm.centre(dve, c - 1)
                        if q == Q_SCALE:
                            norm.scale(dve, c - 1)
                    if not last:
                        for m, j in AT_TAP.get(q, ()):
                            tap(c + 1, 1 - s, m, j)
                        if q == Q_HALO:
                            keep_halo(c + 1)
                        if q == Q_ERR:
                            log_error(c + 1, 1 - s)
                        if q == Q_DT:
                            finish_dt(c + 1, 1 - s)

            dve.wait_ge(a_ready, 1)
            nc.vector.tensor_scalar(a_cols[:], a_cols[:], -1.0, None, ALU.mult).then_inc(a_ready, 1)
            nc.vector.memset(carry[:], 0.0).then_inc(a_ready, 1)
            nc.vector.memset(xin[:, :, 0:HALO], 0.0).then_inc(a_ready, 1)
            dve.wait_ge(a_ready, 4)
            dve.sem_inc(halo_ready, 1)
            dve.sem_inc(h_ready, DEC)
            dve.sem_inc(carry_ready, NU)
            dve.sem_inc(skip_ready, NM)
            dve.sem_inc(norm.z_ready, norm.FREE)
            for m in range(NM):
                for j in range(1, TAPS):
                    tap(0, 0, m, j)
            keep_halo(0)
            log_error(0, 0)
            finish_dt(0, 0)
            over_chunks(dve, NCH, chunk)
            skip(NCH - 1, 1)
            residual(NCH - 1)
            norm.centre(dve, NCH - 1)
            norm.scale(dve, NCH - 1)


def layer1_experts(nc, xT, k, w):
    T = xT.shape[2]
    NCH = T // CH
    BPC = CH // P
    HEADS, DH, E, INNER = 8, 32, w["w1"].shape[1], w["w1"].shape[2]
    assert DH == QUAD and INNER == P and HEADS * DH == 2 * P and HEADS * E == P
    F32R = mybir.dt.float32r
    GROUPS = 2
    HPG = HEADS // GROUPS
    NU = E * GROUPS
    NADD = NU - GROUPS
    HM, UP, EO, PR, WR = 4, 2, 2, 4, 8
    HEAD0, LOGITS, TURN, BACK = GROUPS, GROUPS + HEADS, GROUPS + HEADS + 1, GROUPS + HEADS + 2
    ITEMS = BACK + 1
    Q_OUT, Q_RES, Q_MEAN, Q_CENTRE, Q_SQUARE, Q_VAR, Q_SCALE = 5, 6, 9, 9, 11, 12, 20
    Q_HALF, Q_HIGH, Q_LOW, Q_HEAD, Q_COPY = 0, 0, 1, 4, 5
    Q_LOGITS, Q_KEEP_LOGITS, Q_TURN, Q_MAX, Q_EXP, Q_PICK, Q_BACK, Q_KEEP_WEIGHTS = 13, 13, 15, 16, 17, 18, 25, 25
    with ExitStack() as ctx:
        def sb(name, shape, dt=F32):
            return ctx.enter_context(nc.sbuf_tensor("d_" + name, shape, dt))

        def sem(name):
            return ctx.enter_context(nc.semaphore("d_" + name))

        up_ps = [ctx.enter_context(nc.psum_tensor(f"d_up{i}", [P, 2, CH], F32)) for i in range(UP)]
        eo_ps = [ctx.enter_context(nc.psum_tensor(f"d_eo{i}", [P, CH], F32)) for i in range(EO)]
        work_ps = ctx.enter_context(nc.psum_tensor("d_work", [P, CH], F32))
        norm_ps = ctx.enter_context(nc.psum_tensor("d_norm", [P, CH], F32))
        w_dram = nc.dram_tensor("d_w_scratch", (2, GROUPS, HPG, E, CH), F32, kind="Internal").ap()
        raw = sb("raw", [P, E * INNER])
        emb_raw = sb("emb_raw", [P, E])
        w1 = sb("w1", [P, E, INNER], F32R)
        emb = sb("emb", [P, HEADS, P], F32R)
        w2 = sb("w2", [P, E, DH])
        b1 = sb("b1", [P, E])
        b2 = sb("b2", [P, E])
        heads_w = sb("heads_w", [P, 2, 2 * P])
        heads_b = sb("heads_b", [P, GROUPS])
        sel_raw = sb("sel_raw", [P, HPG, 2, P])
        sel = sb("sel", [P, HPG, 2, P], F32R)
        parts = sb("parts", [P, GROUPS, 2, CH], F32R)
        out_w = sb("out_w", [P, 2, 2 * P])
        out_b = sb("out_b", [P, 2])
        order = sb("order", [P, E])
        heads = sb("heads", [P, 2, HEADS, CH], F32R)
        logit = sb("logit", [P, CH])
        probs = sb("probs", [P, BPC * HEADS, E])
        key = sb("key", [P, BPC * HEADS, E])
        mask = sb("mask", [P, BPC * HEADS, E])
        stat = sb("stat", [P, BPC * HEADS])
        w_t = sb("w_t", [P, CH])
        w_rep = sb("w_rep", [P, WR, CH])
        hmid = sb("hmid", [P, HM, 2, CH])
        prod = sb("prod", [P, PR, CH])
        acc = sb("acc", [P, 2, GROUPS, CH])

        heads_loaded = sem("heads_loaded")
        loaded = sem("loaded")
        sel_ready = sem("sel_ready")
        split_ready = sem("split_ready")
        work_ready = sem("work_ready")
        high_ready = sem("high_ready")
        low_ready = sem("low_ready")
        head_ready = sem("head_ready")
        logit_kept = sem("logit_kept")
        route = sem("route")
        picked = sem("picked")
        emb_ready = sem("emb_ready")
        exp_ready = sem("exp_ready")
        wt_ready = sem("wt_ready")
        w_stored = sem("w_stored")
        w_loaded = [sem(f"w_loaded{i}") for i in range(WR)]
        up_ready = sem("up_ready")
        gelu_ready = sem("gelu_ready")
        down_ready = sem("down_ready")
        prod_ready = sem("prod_ready")
        add_ready = sem("add_ready")
        out_ready = sem("out_ready")
        norm = Norm(nc, sb, sem, norm_ps[:], k, xT)
        ROUTE, PICKS = 11, 7
        NSPLIT = 6

        block = ctx.enter_context(nc.Block())
        LOADS = 8 * 16

        @block.sync
        def _(sp):
            sp.dma_start(heads_w[:], w["heads_w"].rearrange("(h p) m -> p h m", p=P)).then_inc(heads_loaded, 16)
            sp.dma_start(heads_b[:], w["heads_b"]).then_inc(heads_loaded, 16)
            sp.dma_start(sel_raw[:], w["sel"]).then_inc(heads_loaded, 16)
            sp.dma_start(raw[:], w["w1"].rearrange("p e i -> p (e i)")).then_inc(loaded, 16)
            sp.dma_start(emb_raw[:], w["emb"]).then_inc(loaded, 16)
            sp.dma_start(order[:], w["order"]).then_inc(loaded, 16)
            sp.dma_start(w2[:], w["w2"]).then_inc(loaded, 16)
            sp.dma_start(b1[:], w["b1"]).then_inc(loaded, 16)
            sp.dma_start(b2[:], w["b2"]).then_inc(loaded, 16)
            sp.dma_start(out_w[:], w["out_w"].rearrange("(h p) m -> p h m", p=P)).then_inc(loaded, 16)
            sp.dma_start(out_b[:], w["out_b"]).then_inc(loaded, 16)

            def store_weights(c, s):
                sp.wait_ge(wt_ready, c + 1)
                sp.dma_start(w_dram[s].rearrange("g j e t -> (g j e) t"), w_t[:]).then_inc(w_stored, 16)

            def spread(c, s, q):
                if q == 0:
                    sp.wait_ge(w_stored, c * 16 + 16)
                if not (isinstance(c, int) and c == 0 and q < WR):
                    sp.wait_ge(prod_ready, c * NU + q - WR + 1 + EO)
                src = w_dram[s, q % GROUPS, :, q // GROUPS, :].unsqueeze(1).broadcast_to([HPG, DH, CH])
                sp.dma_start(w_rep[:, q % WR], src).then_inc(w_loaded[q % WR], 16)

            def chunk(c, s, first, last):
                for q in range(NU):
                    spread(c, s, q)
                if not last:
                    store_weights(c + 1, 1 - s)
                if not first:
                    store_out(c - 1)

            def store_out(c):
                sp.wait_ge(norm.x_ready, c * 2 + 2)
                sp.dma_start(k["out"][:, :, bass.ts(c, CH)], xT[:, :, bass.ts(c, CH)]).then_inc(k["stored"], 16)

            store_weights(0, 0)
            over_chunks(sp, NCH, chunk)
            store_out(NCH - 1)
            sp.wait_ge(k["stored"], NCH * 16)

        @block.tensor
        def _(pe):
            def product(c, s, i):
                if i == 0:
                    pe.wait_ge(wt_ready, c)
                elif i <= HEAD0:
                    pe.wait_ge(high_ready, c * GROUPS + i)
                    pe.wait_ge(low_ready, c * GROUPS + i)
                elif i <= LOGITS:
                    pe.wait_ge(head_ready, c * HEADS + i - HEAD0)
                if i < HEAD0:
                    for half in range(2):
                        last = nc.tensor.matmul(work_ps[:], heads_w[:, half, i * P:(i + 1) * P],
                                                xT[:, half, bass.ts(c, CH)],
                                                start=(half == 0), stop=(half == 1))
                elif i < LOGITS:
                    g, j = (i - HEAD0) // HPG, (i - HEAD0) % HPG
                    for part in range(2):
                        last = nc.tensor.matmul(work_ps[:], sel[:, j, part, :], parts[:, g, part, :],
                                                start=(part == 0), stop=(part == 1))
                elif i == LOGITS:
                    for g in range(HEADS):
                        last = nc.tensor.matmul(work_ps[:], emb[:, g, :], heads[:, s, g, :],
                                                start=(g == 0), stop=(g == HEADS - 1))
                elif i == TURN:
                    pe.wait_ge(logit_kept, c + 1)
                    for b in range(BPC):
                        last = nc.tensor.transpose(work_ps[:, b * P:(b + 1) * P], logit[:, b * P:(b + 1) * P],
                                                   k["ident"])
                else:
                    pe.wait_ge(route, (c + 1) * ROUTE)
                    for b in range(BPC):
                        last = nc.tensor.transpose(
                            work_ps[:, b * P:(b + 1) * P],
                            probs[:, b * HEADS:(b + 1) * HEADS, :].rearrange("p g e -> p (g e)"), k["ident"])
                last.then_inc(work_ready, 1)

            def up(c, s, q, r):
                e, g = q // GROUPS, q % GROUPS
                if q == 0 and r == 0:
                    pe.wait_ge(head_ready, (c + 1) * HEADS)
                pe.wait_ge(gelu_ready, c * 2 * NU + 2 * q + r + 1)
                for j in range(2):
                    last = nc.tensor.matmul(up_ps[r][:, j, :], w1[:, e, :], heads[:, s, g * HPG + 2 * r + j, :],
                                            start=True, stop=True)
                last.then_inc(up_ready, 1)

            def down(c, q, r):
                e = q // GROUPS
                pe.wait_ge(gelu_ready, c * 2 * NU + 2 * q + r + 1 + UP)
                if r == 0:
                    pe.wait_ge(prod_ready, c * NU + q + 1)
                for j in (2 * r, 2 * r + 1):
                    last = nc.tensor.matmul(eo_ps[q % EO][j * DH:(j + 1) * DH, :], w2[:, e, :],
                                            hmid[:, (2 * q + r) % HM, j % 2, :], start=True, stop=True)
                if r == 1:
                    last.then_inc(down_ready, 1)

            def project_out(c, s, half):
                if half == 0:
                    pe.wait_ge(add_ready, (c + 1) * NADD)
                    pe.wait_ge(norm.log_ready, c)
                else:
                    pe.wait_ge(norm.z_ready, c * 2 + 1 + norm.FREE)
                for g in range(GROUPS):
                    last = nc.tensor.matmul(norm_ps[:], out_w[:, g, half * P:(half + 1) * P], acc[:, s, g, :],
                                            start=(g == 0), stop=(g == GROUPS - 1))
                last.then_inc(out_ready, 1)

            def chunk(c, s, first, last):
                for q in range(NU):
                    for r in range(2):
                        up(c, s, q, r)
                        if q >= 1:
                            down(c, q - 1, r)
                        elif not first:
                            down(c - 1, NU - 1, r)
                    if not first:
                        if q in (Q_OUT, Q_OUT + 2):
                            project_out(c - 1, 1 - s, (q - Q_OUT) // 2)
                        if q == Q_MEAN:
                            norm.mean(pe, c - 1)
                        if q == Q_VAR:
                            norm.variance(pe, c - 1)
                    if not last:
                        if q in (Q_HALF, Q_HALF + 2):
                            product(c + 1, 1 - s, (q - Q_HALF) // 2)
                        if Q_HEAD <= q < Q_HEAD + HEADS:
                            product(c + 1, 1 - s, HEAD0 + q - Q_HEAD)
                        if q == Q_LOGITS:
                            product(c + 1, 1 - s, LOGITS)
                        if q == Q_TURN:
                            product(c + 1, 1 - s, TURN)
                        if q == Q_BACK:
                            product(c + 1, 1 - s, BACK)

            pe.sem_inc(down_ready, HM // 2)
            pe.wait_ge(heads_loaded, 3 * 16)
            for i in range(ITEMS):
                if i == HEAD0:
                    pe.wait_ge(sel_ready, 1)
                if i == LOGITS:
                    pe.wait_ge(split_ready, NSPLIT)
                    pe.wait_ge(emb_ready, 3 * HEADS)
                product(0, 0, i)
            over_chunks(pe, NCH, chunk)
            down(NCH - 1, NU - 1, 0)
            down(NCH - 1, NU - 1, 1)
            project_out(NCH - 1, 1, 0)
            project_out(NCH - 1, 1, 1)
            norm.mean(pe, NCH - 1)
            norm.variance(pe, NCH - 1)

        @block.scalar
        def _(act):
            def high(c, g):
                act.wait_ge(work_ready, c * ITEMS + g + 1)
                nc.scalar.activation(parts[:, g, 0, :], work_ps[:], ACT.Identity, bias=heads_b[:, g:g + 1]
                                     ).then_inc(high_ready, 1)

            def keep_logits(c):
                act.wait_ge(work_ready, c * ITEMS + LOGITS + 1)
                nc.scalar.copy(logit[:], work_ps[:]).then_inc(logit_kept, 1)

            def exp(c):
                act.wait_ge(route, c * ROUTE + 2)
                nc.scalar.activation(probs[:], probs[:], ACT.Exp).then_inc(exp_ready, 1)

            def keep_weights(c):
                act.wait_ge(work_ready, (c + 1) * ITEMS)
                act.wait_ge(w_stored, c * 16)
                nc.scalar.copy(w_t[:], work_ps[:]).then_inc(wt_ready, 1)

            def chunk(c, s, first, last):
                for q in range(NU):
                    e = q // GROUPS
                    for r in range(2):
                        act.wait_ge(up_ready, c * 2 * NU + 2 * q + r + 1)
                        if r == 0:
                            act.wait_ge(down_ready, c * NU + q + 1)
                        nc.scalar.activation(hmid[:, (2 * q + r) % HM], up_ps[r][:], ACT.Gelu,
                                             bias=b1[:, e:e + 1]).then_inc(gelu_ready, 1)
                    if not first:
                        if q == Q_SQUARE:
                            norm.square(act, c - 1)
                    if q == Q_EXP:
                        if not first:
                            norm.deviation(act, c - 1)
                        if not last:
                            exp(c + 1)
                    if not last:
                        if q in (Q_HIGH, Q_HIGH + 2):
                            high(c + 1, (q - Q_HIGH) // 2)
                        if q == Q_KEEP_LOGITS:
                            keep_logits(c + 1)
                        if q == Q_KEEP_WEIGHTS:
                            keep_weights(c + 1)

            act.wait_ge(heads_loaded, 3 * 16)
            act.sem_inc(gelu_ready, UP)
            for g in range(GROUPS):
                high(0, g)
            act.wait_ge(loaded, LOADS)
            keep_logits(0)
            exp(0)
            keep_weights(0)
            over_chunks(act, NCH, chunk)
            norm.square(act, NCH - 1)
            norm.deviation(act, NCH - 1)

        @block.gpsimd
        def _(pool):
            def chunk(c, s, first, last):
                for q in range(GROUPS, NU):
                    g = q % GROUPS
                    pool.wait_ge(prod_ready, c * NU + q + 1 + EO)
                    if q >= 2 * GROUPS:
                        pool.wait_ge(add_ready, c * NADD + q - 2 * GROUPS + 1)
                    nc.gpsimd.tensor_tensor(acc[:, s, g, :], acc[:, s, g, :], prod[:, q % PR, :], ALU.add
                                            ).then_inc(add_ready, 1)

            over_chunks(pool, NCH, chunk)

        @block.vector
        def _(dve):
            def low(c, g):
                dve.wait_ge(high_ready, c * GROUPS + g + 1)
                nc.vector.scalar_tensor_tensor(out=parts[:, g, 1, :], in0=work_ps[:], scalar=heads_b[:, g:g + 1],
                                               in1=parts[:, g, 0, :].bitcast(F32),
                                               op0=ALU.add, op1=ALU.subtract).then_inc(low_ready, 1)

            def keep_head(c, s, i):
                dve.wait_ge(work_ready, c * ITEMS + HEAD0 + i + 1)
                nc.vector.tensor_copy(heads[:, s, i, :], work_ps[:]).then_inc(head_ready, 1)

            def per_head(a):
                return a.unsqueeze(2).broadcast_to([P, BPC * HEADS, E])

            def step(c, n, ins):
                ins.then_inc(route, 1)
                dve.wait_ge(route, c * ROUTE + n)

            def route_max(c):
                dve.wait_ge(work_ready, c * ITEMS + TURN + 1)
                turned = work_ps[:].rearrange("p (g e) -> p g e", e=E)
                step(c, 1, nc.vector.reduce_max(stat[:], turned, axis=AX_X))
                step(c, 2, nc.vector.tensor_tensor(probs[:], turned, per_head(stat[:]), ALU.subtract))

            def route_pick(c, n):
                if n == 0:
                    dve.wait_ge(exp_ready, c + 1)
                    step(c, 3, nc.vector.reduce_sum(stat[:], probs[:], axis=AX_X))
                    step(c, 4, nc.vector.reciprocal(stat[:], stat[:]))
                elif n == 1:
                    step(c, 5, nc.vector.tensor_tensor(probs[:], probs[:], per_head(stat[:]), ALU.mult))
                elif n == 2:
                    step(c, 6, nc.vector.tensor_tensor(
                        key[:], probs[:], order[:].unsqueeze(1).broadcast_to([P, BPC * HEADS, E]), ALU.mult))
                elif n == 3:
                    step(c, 7, nc.vector.reduce_max(stat[:], key[:], axis=AX_X))
                elif n == 4:
                    step(c, 8, nc.vector.tensor_tensor(mask[:], key[:], per_head(stat[:]), ALU.is_lt))
                    step(c, 9, nc.vector.tensor_tensor(mask[:], mask[:], key[:], ALU.mult))
                elif n == 5:
                    step(c, 10, nc.vector.reduce_max(stat[:], mask[:], axis=AX_X))
                else:
                    nc.vector.tensor_tensor(mask[:], key[:], per_head(stat[:]), ALU.is_ge).then_inc(picked, 1)
                    dve.wait_ge(picked, c + 1)
                    step(c, 11, nc.vector.tensor_tensor(probs[:], probs[:], mask[:], ALU.mult))

            def weigh(c, s, q):
                e, g = q // GROUPS, q % GROUPS
                dve.wait_ge(w_loaded[q % WR], (c * (NU // WR) + q // WR + 1) * 16)
                dve.wait_ge(down_ready, c * NU + q + 1 + HM // 2)
                if q < GROUPS:
                    out = acc[:, s, g, :]
                else:
                    dve.wait_ge(add_ready, c * NADD + max(q - PR - GROUPS + 1, 0))
                    out = prod[:, q % PR, :]
                nc.vector.scalar_tensor_tensor(out=out, in0=eo_ps[q % EO][:], scalar=b2[:, e:e + 1],
                                               in1=w_rep[:, q % WR, :], op0=ALU.add, op1=ALU.mult
                                               ).then_inc(prod_ready, 1)

            def residual(c, half):
                dve.wait_ge(out_ready, c * 2 + half + 1)
                norm.add_residual(dve, c, half, norm_ps[:], out_b[:, half:half + 1])

            def chunk(c, s, first, last):
                for q in range(NU + 1):
                    if not last:
                        if q in (Q_LOW, Q_LOW + 2):
                            low(c + 1, (q - Q_LOW) // 2)
                        if Q_COPY <= q < Q_COPY + HEADS:
                            keep_head(c + 1, 1 - s, q - Q_COPY)
                    if q >= 1:
                        weigh(c, s, q - 1)
                    if not first:
                        if q in (Q_RES, Q_RES + 2):
                            residual(c - 1, (q - Q_RES) // 2)
                        if q == Q_CENTRE:
                            norm.centre(dve, c - 1)
                        if q == Q_SCALE:
                            norm.scale(dve, c - 1)
                    if not last:
                        if q == Q_MAX:
                            route_max(c + 1)
                        if Q_PICK <= q < Q_PICK + PICKS:
                            route_pick(c + 1, q - Q_PICK)

            def split_weights(n):
                if n == 0:
                    dve.wait_ge(loaded, LOADS)
                    nc.vector.memset(emb[:].bitcast(F32), 0.0).then_inc(split_ready, 1)
                    nc.vector.tensor_copy(w1[:], raw[:].rearrange("p (e i) -> p e i", e=E)).then_inc(split_ready, 1)
                elif n == 1:
                    dve.wait_ge(split_ready, 2)
                    for g in range(HEADS):
                        nc.vector.tensor_copy(emb[:, g, g * E:(g + 1) * E], emb_raw[:]).then_inc(emb_ready, 1)
                elif n < 4:
                    i = (1, 3)[n - 2]
                    rows = slice(i * DH, (i + 1) * DH)
                    dve.wait_ge(emb_ready, HEADS)
                    nc.vector.tensor_tensor(w1[rows], raw[rows].rearrange("p (e i) -> p e i", e=E),
                                            w1[rows].bitcast(F32), ALU.subtract).then_inc(split_ready, 1)
                    nc.vector.tensor_tensor(emb_raw[rows], emb_raw[rows], emb[rows, 0, 0:E].bitcast(F32),
                                            ALU.subtract).then_inc(split_ready, 1)
                else:
                    dve.wait_ge(split_ready, NSPLIT)
                    for i in (1, 3):
                        rows = slice(i * DH, (i + 1) * DH)
                        for g in range(HEADS):
                            nc.vector.tensor_copy(emb[rows, g, g * E:(g + 1) * E], emb_raw[rows]).then_inc(emb_ready, 1)

            dve.wait_ge(heads_loaded, 3 * 16)
            nc.vector.tensor_copy(sel[:], sel_raw[:]).then_inc(sel_ready, 1)
            dve.sem_inc(prod_ready, EO)
            dve.sem_inc(norm.z_ready, norm.FREE)
            split_weights(0)
            low(0, 0)
            split_weights(1)
            low(0, 1)
            for i in range(HEADS):
                if i < 3:
                    split_weights(2 + i)
                keep_head(0, 0, i)
            dve.wait_ge(emb_ready, 3 * HEADS)
            route_max(0)
            for n in range(PICKS):
                route_pick(0, n)
            over_chunks(dve, NCH, chunk)
            residual(NCH - 1, 0)
            residual(NCH - 1, 1)
            norm.centre(dve, NCH - 1)
            norm.scale(dve, NCH - 1)


def build(nc, d, T):
    with ExitStack() as ctx:
        def sb(name, shape):
            return ctx.enter_context(nc.sbuf_tensor(name, shape, F32))

        xT = sb("xT", [P, 2, T])
        sel_rep = sb("sel_rep", [P, KPQ, P])
        sel_sum = sb("sel_sum", [P, KPQ, QUAD])
        avg = sb("avg", [P, P])
        eps = sb("eps", [P, 1])
        ident = sb("ident", [P, P])
        loaded = ctx.enter_context(nc.semaphore("x_loaded"))
        rest_loaded = ctx.enter_context(nc.semaphore("x_rest_loaded"))
        stored = ctx.enter_context(nc.semaphore("x_stored"))
        k = {"sel_rep": sel_rep, "sel_sum": sel_sum, "avg": avg[:], "eps": eps[:], "ident": ident[:],
             "rest_loaded": rest_loaded, "out": d["out"].rearrange("(h p) t -> p h t", p=P), "stored": stored}
        with nc.Block() as block:
            @block.vector
            def _(dve):
                nc.vector.memset(eps[:], EPS)

            @block.sync
            def _(sp):
                x = d["xT"].rearrange("(h p) t -> p h t", p=P)
                sp.dma_start(xT[:, :, 0:2 * CH], x[:, :, 0:2 * CH]).then_inc(loaded, 16)
                sp.dma_start(sel_rep[:], d["sel_rep"]).then_inc(loaded, 16)
                sp.dma_start(sel_sum[:], d["sel_sum"]).then_inc(loaded, 16)
                sp.dma_start(avg[:], d["avg"]).then_inc(loaded, 16)
                sp.dma_start(ident[:], d["ident"]).then_inc(loaded, 16)
                sp.dma_start(xT[:, :, 2 * CH:], x[:, :, 2 * CH:]).then_inc(rest_loaded, 16)
                sp.wait_ge(loaded, 5 * 16)
        layer0_scan(nc, xT, k, {n[2:]: a for n, a in d.items() if n.startswith("a_")})
        with ExitStack() as scan_ctx:
            of_scan = {n[2:]: a for n, a in d.items() if n.startswith("c_")}
            weights = ScanWeights(nc, scan_ctx, of_scan)
            layer0_experts(nc, xT, k, {n[2:]: a for n, a in d.items() if n.startswith("b_")}, weights)
            layer1_scan(nc, xT, k, of_scan, weights)
        layer1_experts(nc, xT, k, {n[2:]: a for n, a in d.items() if n.startswith("d_")})


def kernel(**inputs):
    import numpy as np
    import concourse.bacc as bacc
    from concourse.bass_utils import run_bass_kernel_spmd

    D = inputs["L0_attn_sequence"].shape[2]
    T = inputs["L0_attn_sequence"].shape[1]
    x = {n: np.asarray(a) for n, a in inputs.items()}

    def scan_cols(a):
        return a.reshape(-1, NQ, KPQ, P).transpose(3, 0, 2, 1).reshape(P, -1)

    def cols(a):
        return a.reshape(-1, P).T

    row = np.arange(P)
    sel_rep = np.zeros((P, KPQ, P), np.float32)
    sel_sum = np.zeros((P, KPQ, QUAD), np.float32)
    for kk in range(KPQ):
        sel_rep[:, kk, :] = (row[:, None] % QUAD) == (row[None, :] // N_STATE + DPT * kk)
        sel_sum[:, kk, :] = (row[:, None] // N_STATE + DPT * kk) == np.arange(QUAD)[None, :]
    sel_parts = np.zeros((P, NQ, 2, P), np.float32)
    for j in range(NQ):
        for part in range(2):
            sel_parts[:, j, part, :] = ((row[:, None] // QUAD == j) & (row[None, :] // (2 * QUAD) == part)
                                        & (row[:, None] % QUAD == row[None, :] % QUAD))
    w_bc = np.stack([np.tile(x["L0_attn_W_B"].T, (1, DPT)), np.tile(x["L0_attn_W_C"].T, (1, DPT)),
                     np.tile(x["L0_attn_W_Delta"].T, (1, P))], axis=1)
    def with_shared(name):
        return np.concatenate([x["L0_ffn_" + name], x["L0_ffn_" + name + "_s"][None]])

    def halves(a):
        return a.reshape(a.shape[0], 2, P, a.shape[2]).transpose(0, 2, 1, 3).reshape(a.shape[0], P, -1)

    experts = np.concatenate([halves(with_shared("Wg")), halves(with_shared("Wu")), with_shared("Wd"),
                              with_shared("bg")[:, :, None], with_shared("bu")[:, :, None]], axis=2)
    arrays = {
        "xT": x["L0_attn_sequence"][0].T,
        "sel_rep": sel_rep, "sel_sum": sel_sum, "avg": np.full((P, P), 1.0 / D, np.float32),
        "ident": np.eye(P, dtype=np.float32),
        "a_w_bc": w_bc, "a_x": x["L0_attn_sequence"][0].T,
        "a_b_b": np.tile(x["L0_attn_b_B"], DPT)[:, None], "a_b_c": np.tile(x["L0_attn_b_C"], DPT)[:, None],
        "a_b_step": np.tile(x["L0_attn_b_Delta"], P)[:, None],
        "a_bias_step": np.tile(x["L0_attn_bias_Delta"], P)[:, None],
        "a_a_cols": scan_cols(x["L0_attn_A"]),
        "b_router_w": x["L0_ffn_Wr"], "b_router_b": x["L0_ffn_br"][:, None],
        "b_down_b": np.concatenate([x["L0_ffn_bd"], x["L0_ffn_bd_s"][None]]),
        "b_experts": experts,
        "c_in_w": x["L1_attn_in_proj_w"].T, "c_x_w": x["L1_attn_x_proj_w"].T,
        "c_dt_w": x["L1_attn_dt_proj_w"].T, "c_out_w": x["L1_attn_out_proj_w"].T,
        "c_conv_w": x["L1_attn_conv_w"].reshape(-1, P, x["L1_attn_conv_w"].shape[1]).transpose(1, 0, 2),
        "c_vecs": np.stack([cols(x["L1_attn_conv_b"]), cols(x["L1_attn_dt_proj_b"]),
                            cols(x["L1_attn_D_param"])], axis=1),
        "d_w1": np.tile(x["L1_ffn_W1"].transpose(1, 0, 2), (4, 1, 1)),
        "d_emb": np.tile(x["L1_ffn_expert_emb"], (4, 1)),
        "d_w2": x["L1_ffn_W2"].transpose(1, 0, 2), "d_b1": x["L1_ffn_b1"].T,
        "d_b2": np.tile(x["L1_ffn_b2"].T, (4, 1)),
        "d_heads_w": x["L1_ffn_Wm"], "d_heads_b": cols(x["L1_ffn_bm"]), "d_sel": sel_parts,
        "d_out_w": x["L1_ffn_Wo"], "d_out_b": cols(x["L1_ffn_bo"]),
        "d_order": np.tile((1.0 + np.arange(15, -1, -1) * 2.0**-22).astype(np.float32), (P, 1)),
        "c_a_log_cols": x["L1_attn_A_log"].reshape(-1, P, N_STATE).transpose(1, 2, 0).reshape(P, -1),
    }
    nc = bacc.Bacc("TRN2", target_bir_lowering=False, num_devices=1)
    arrays = {n: np.ascontiguousarray(a) for n, a in arrays.items()}
    d = {n: nc.dram_tensor("in_" + n, a.shape, mybir.dt.from_np(a.dtype), kind="ExternalInput").ap()
         for n, a in arrays.items()}
    d["out"] = nc.dram_tensor("out_0", (D, T), F32, kind="ExternalOutput").ap()
    build(nc, d, T)
    r = run_bass_kernel_spmd(nc, [{"in_" + n: a for n, a in arrays.items()}], core_ids=[0])
    return np.ascontiguousarray(r.results[0]["out_0"].T)[None]
```
